# Optimizing a Trainium2 kernel written in Bass

```python
import numpy as np
import jax
import jax.numpy as jnp

def _softmax(x, axis=-1):
    return jax.nn.softmax(x, axis=axis)

def _gelu(x):
    return jax.nn.gelu(x, approximate=True)

def _silu(x):
    return jax.nn.silu(x)

def _sigmoid(x):
    return jax.nn.sigmoid(x)

def _layernorm(x, axis=-1, eps=1e-05):
    m = jnp.mean(x, axis=axis, keepdims=True)
    v = jnp.var(x, axis=axis, keepdims=True)
    return (x - m) / jnp.sqrt(v + eps)

def _scatter_add(tgt, idx, src, axis=0):
    return tgt.at[idx].add(src)

def _segment_sum(src, seg, n):
    return jax.ops.segment_sum(src, seg, n)
kernel_name = 'mk_decoder_postln_d2_seqx_r4_8726a9'

def setup_inputs(seed: int=0):
    np.random.seed(seed)
    _w = jnp.asarray

    def _rec_inputs():
        import jax
        import jax.numpy as jnp
        _rk = jax.random.key(seed)
        x = -0.0005146 + 1 * jax.random.normal(jax.random.fold_in(_rk, 1), (4, 512, 256), jnp.float32)
        _lenS = 512 - jax.random.randint(jax.random.fold_in(_rk, 7), (4,), 0, max(1, 512 // 4) + 1, jnp.int32)
        _lenS2 = 64 - jax.random.randint(jax.random.fold_in(_rk, 8), (4,), 0, max(1, 64 // 4) + 1, jnp.int32)
        _ctx_768P = jax.random.normal(jax.random.fold_in(_rk, 11), (4, 16, 192), jnp.float32)
        _ctx_768c = jax.random.dirichlet(jax.random.fold_in(_rk, 511), 0.3 * jnp.ones((16,), jnp.float32), (4, 64))
        _ctx_768t = jnp.einsum('bsk,bkd->bsd', _ctx_768c, _ctx_768P)
        _ctx_768t = _ctx_768t * jax.lax.rsqrt(jnp.mean(jnp.square(_ctx_768t)) + 1e-12) * 0.953939
        ctx_768 = -0.00040386 + 0.999972 * (_ctx_768t + 0.3 * jax.random.normal(jax.random.fold_in(_rk, 611), (4, 64, 192), jnp.float32))
        _validS = jnp.arange(512)[None, :] < _lenS[:, None]
        _validS2 = jnp.arange(64)[None, :] < _lenS2[:, None]
        _causal = jnp.tril(jnp.ones((512, 512), dtype=bool))
        mask_BxS2_bk0 = jnp.logical_not(jnp.broadcast_to(_validS2[:, :], (4, 64)))
        mask_BxS_bf1 = jnp.ones((4, 512), dtype=bool)
        mask_BxS2_bf1 = jnp.ones((4, 64), dtype=bool)
        return (x, ctx_768, mask_BxS2_bk0, mask_BxS_bf1, mask_BxS2_bf1)
    x, ctx_768, mask_BxS2_bk0, mask_BxS_bf1, mask_BxS2_bf1 = _rec_inputs()

    def _L0_attn_setup():
        import jax, jax.numpy as jnp
        import numpy as np
        D_MODEL = 256
        NUM_HEADS = 16
        D_K = D_MODEL // NUM_HEADS
        key = jax.random.key(seed)
        k1, k2, k3, k4, k5 = jax.random.split(key, 5)
        scale = 1.0 / np.sqrt(D_MODEL)
        x = jax.random.normal(k1, (2, 2048, D_MODEL), dtype=jnp.float32)
        W_qkv = jax.random.normal(k2, (D_MODEL, 3 * D_MODEL), dtype=jnp.float32) * scale
        b_qkv = jax.random.normal(k3, (3 * D_MODEL,), dtype=jnp.float32) * 0.01
        W_out = jax.random.normal(k4, (D_MODEL, D_MODEL), dtype=jnp.float32) * scale
        b_out = jax.random.normal(k5, (D_MODEL,), dtype=jnp.float32) * 0.01
        return {'x': x, 'W_qkv': W_qkv, 'b_qkv': b_qkv, 'W_out': W_out, 'b_out': b_out}
    _L0_attn_all = _L0_attn_setup()
    _L0_attn_in = {k: v for k, v in _L0_attn_all.items() if k in ('W_qkv', 'b_qkv', 'W_out', 'b_out')}
    del _L0_attn_all

    def _L0_xattn_setup():
        import jax, jax.numpy as jnp
        import numpy as np
        DIM_IN, DIM_LAT, DIM_HEAD = (192, 256, 64)
        INNER = max(DIM_LAT, DIM_IN)
        HEADS = INNER // DIM_HEAD
        SCALE = DIM_HEAD ** (-0.5)
        RMS_EPS = 1e-08
        LN_EPS = 1e-05

        def layernorm(x, g, b):
            mu = jnp.mean(x, axis=-1, keepdims=True)
            var = jnp.mean((x - mu) ** 2, axis=-1, keepdims=True)
            return (x - mu) * jax.lax.rsqrt(var + LN_EPS) * g + b

        def rmsnorm(x, gamma):
            norm = jnp.sqrt(jnp.sum(x * x, axis=-1, keepdims=True)) * x.shape[-1] ** (-0.5)
            return x / jnp.maximum(norm, RMS_EPS) * gamma
        key = jax.random.key(seed)
        ks = jax.random.split(key, 12)
        b, n, m = (4, 1024, 128)
        x = jax.random.normal(ks[0], (b, n, DIM_IN), jnp.float32)
        latents = jax.random.normal(ks[1], (b, m, DIM_LAT), jnp.float32)
        mask = jax.random.randint(ks[2], (b, n), 0, 2).astype(bool)
        s = lambda k, sh, fan: jax.random.normal(k, sh, jnp.float32) * fan ** (-0.5)
        return {'x': x, 'latents': latents, 'mask': mask, 'ln_x_g': jnp.ones((DIM_IN,), jnp.float32), 'ln_x_b': jnp.zeros((DIM_IN,), jnp.float32), 'ln_l_g': jnp.ones((DIM_LAT,), jnp.float32), 'ln_l_b': jnp.zeros((DIM_LAT,), jnp.float32), 'qn_g': jnp.ones((DIM_HEAD,), jnp.float32), 'kn_g': jnp.ones((DIM_HEAD,), jnp.float32), 'Wq': s(ks[3], (INNER, DIM_LAT), DIM_LAT), 'Wkv': s(ks[4], (2 * INNER, DIM_IN), DIM_IN), 'Wlkv': s(ks[5], (2 * INNER, DIM_LAT), DIM_LAT), 'Wo': s(ks[6], (DIM_LAT, INNER), INNER), 'bo': jnp.zeros((DIM_LAT,), jnp.float32)}
    _L0_xattn_all = _L0_xattn_setup()
    _L0_xattn_in = {k: v for k, v in _L0_xattn_all.items() if k in ('ln_x_g', 'ln_x_b', 'ln_l_g', 'ln_l_b', 'qn_g', 'kn_g', 'Wq', 'Wkv', 'Wlkv', 'Wo', 'bo')}
    del _L0_xattn_all

    def _L0_ffn_setup():
        import jax, jax.numpy as jnp
        import numpy as np
        B, S, H, E, F = (2, 512, 256, 8, 1024)
        key = jax.random.key(seed)
        k1, k2, k3, k4 = jax.random.split(key, 4)
        h = jax.random.normal(k1, (B, S, H), dtype=jnp.float32)
        Wr = jax.random.normal(k2, (H, E), dtype=jnp.float32) / np.sqrt(H)
        W1 = jax.random.normal(k3, (E, H, F), dtype=jnp.float32) / np.sqrt(H)
        W2 = jax.random.normal(k4, (E, F, H), dtype=jnp.float32) / np.sqrt(F)
        return {'h': h, 'Wr': Wr, 'W1': W1, 'W2': W2}
    _L0_ffn_all = _L0_ffn_setup()
    _L0_ffn_in = {k: v for k, v in _L0_ffn_all.items() if k in ('Wr', 'W1', 'W2')}
    del _L0_ffn_all

    def _L1_attn_setup():
        import jax, jax.numpy as jnp
        import numpy as np
        from jax import lax
        B, N, DIM = (2, 512, 256)
        HEADS, DHEAD = (16, 64)
        NUM_MEM_KV = 16
        SPARSE_TOPK = 64
        INNER = HEADS * DHEAD
        key = jax.random.key(seed)
        ks = jax.random.split(key, 10)
        s = 0.02
        return {'x': jax.random.normal(ks[0], (B, N, DIM), dtype=jnp.float32), 'Wq': jax.random.normal(ks[1], (DIM, INNER), dtype=jnp.float32) * s, 'Wk': jax.random.normal(ks[2], (DIM, INNER), dtype=jnp.float32) * s, 'Wv': jax.random.normal(ks[3], (DIM, INNER), dtype=jnp.float32) * s, 'pre_proj': jax.random.normal(ks[4], (HEADS, HEADS), dtype=jnp.float32), 'post_proj': jax.random.normal(ks[5], (HEADS, HEADS), dtype=jnp.float32), 'mem_k': jax.random.normal(ks[6], (HEADS, NUM_MEM_KV, DHEAD), dtype=jnp.float32), 'mem_v': jax.random.normal(ks[7], (HEADS, NUM_MEM_KV, DHEAD), dtype=jnp.float32), 'Wo': jax.random.normal(ks[8], (INNER, DIM), dtype=jnp.float32) * s, 'bo': jnp.zeros((DIM,), dtype=jnp.float32)}
    _L1_attn_all = _L1_attn_setup()
    _L1_attn_in = {k: v for k, v in _L1_attn_all.items() if k in ('Wq', 'Wk', 'Wv', 'pre_proj', 'post_proj', 'mem_k', 'mem_v', 'Wo', 'bo')}
    del _L1_attn_all

    def _L1_xattn_setup():
        import jax, jax.numpy as jnp
        import numpy as np
        B, T, DT, G, DV = (16, 128, 256, 144, 192)
        H, DH = (4, 32)
        INNER = H * DH
        HID = 4 * DT
        N_STATE = 64
        K_TOP = 32

        def layernorm(x, g, b, eps=1e-05):
            m = x.mean(-1, keepdims=True)
            v = x.var(-1, keepdims=True)
            return (x - m) * jax.lax.rsqrt(v + eps) * g + b

        def s4d(x, log_dt, A_re, A_im, C_re, C_im, D_skip):
            Bb, L, D = x.shape
            dt = jnp.exp(log_dt)
            A = A_re + 1j * A_im
            C = C_re + 1j * C_im
            dtA = dt[:, None] * A
            dC = C * (jnp.exp(dtA) - 1.0) / A
            powers = jnp.exp(dtA[:, :, None] * jnp.arange(L))
            K = 2.0 * jnp.einsum('dn,dnl->dl', dC, powers).real
            n = 2 * L
            Kf = jnp.fft.rfft(K, n=n, axis=-1)
            xf = jnp.fft.rfft(x, n=n, axis=1)
            y = jnp.fft.irfft(xf * Kf.T[None], n=n, axis=1)[:, :L]
            return y + x * D_skip
        key = jax.random.key(seed)
        ks = jax.random.split(key, 16)
        s = 0.02
        inp = {'x_text': jax.random.normal(ks[0], (B, T, DT), jnp.float32), 'x_vision': jax.random.normal(ks[1], (B, G, DV), jnp.float32), 'text_mask': jnp.ones((B, T), bool), 'vision_mask': jnp.ones((B, G), bool), 'Wq': jax.random.normal(ks[2], (DT, INNER), jnp.float32) * s, 'Wk': jax.random.normal(ks[3], (DV, INNER), jnp.float32) * s, 'Wv': jax.random.normal(ks[4], (DV, DT), jnp.float32) * s, 'W_film_in': jax.random.normal(ks[5], (DT, 2 * DT), jnp.float32) * s, 'b_film_in': jnp.zeros((2 * DT,), jnp.float32), 'W_film_out': jax.random.normal(ks[6], (DT, 2 * DT), jnp.float32) * s, 'b_film_out': jnp.zeros((2 * DT,), jnp.float32), 'g_norm_in': jnp.ones((DT,), jnp.float32), 'b_norm_in': jnp.zeros((DT,), jnp.float32), 'g_norm_out': jnp.ones((DT,), jnp.float32), 'b_norm_out': jnp.zeros((DT,), jnp.float32), 'g_ffn': jnp.ones((DT,), jnp.float32), 'b_ffn': jnp.zeros((DT,), jnp.float32), 'W1': jax.random.normal(ks[7], (DT, HID), jnp.float32) * s, 'b1': jnp.zeros((HID,), jnp.float32), 'W2': jax.random.normal(ks[8], (HID, DT), jnp.float32) * s, 'b2': jnp.zeros((DT,), jnp.float32), 'log_dt': jnp.log(0.001) + jax.random.uniform(ks[9], (DT,), jnp.float32) * (jnp.log(0.1) - jnp.log(0.001)), 'A_re': -0.5 * jnp.ones((DT, N_STATE), jnp.float32), 'A_im': jnp.tile(jnp.pi * jnp.arange(N_STATE, dtype=jnp.float32), (DT, 1)), 'C_re': jax.random.normal(ks[10], (DT, N_STATE), jnp.float32) * 0.5 ** 0.5, 'C_im': jax.random.normal(ks[11], (DT, N_STATE), jnp.float32) * 0.5 ** 0.5, 'D_skip': jax.random.normal(ks[12], (DT,), jnp.float32), 'mod_gate': jnp.array(0.5, jnp.float32)}
        return inp
    _L1_xattn_all = _L1_xattn_setup()
    _L1_xattn_in = {k: v for k, v in _L1_xattn_all.items() if k in ('Wq', 'Wk', 'Wv', 'W_film_in', 'b_film_in', 'W_film_out', 'b_film_out', 'g_norm_in', 'b_norm_in', 'g_norm_out', 'b_norm_out', 'g_ffn', 'b_ffn', 'W1', 'b1', 'W2', 'b2', 'log_dt', 'A_re', 'A_im', 'C_re', 'C_im', 'D_skip', 'mod_gate')}
    del _L1_xattn_all

    def _L1_ffn_setup():
        import jax, jax.numpy as jnp
        import numpy as np
        B, S, D = (4, 128, 256)
        E, K, H = (64, 8, 64)
        ES, HS = (2, 512)
        key = jax.random.key(seed)
        ks = jax.random.split(key, 8)
        scale = 0.02
        rn = lambda k, shape, s: jax.random.normal(k, shape, jnp.float32) * s
        return {'x': rn(ks[0], (B, S, D), 1.0), 'router_w': rn(ks[1], (D, E), scale), 'router_b': jnp.zeros((E,), jnp.float32), 'w1': rn(ks[2], (E, D, H), scale), 'b1': jnp.zeros((E, H), jnp.float32), 'w2': rn(ks[3], (E, H, D), scale), 'b2': jnp.zeros((E, D), jnp.float32), 'sw1': rn(ks[4], (ES, D, HS), scale), 'sb1': jnp.zeros((ES, HS), jnp.float32), 'sw2': rn(ks[5], (ES, HS, D), scale), 'sb2': jnp.zeros((ES, D), jnp.float32)}
    _L1_ffn_all = _L1_ffn_setup()
    _L1_ffn_in = {k: v for k, v in _L1_ffn_all.items() if k in ('router_w', 'router_b', 'w1', 'b1', 'w2', 'b2', 'sw1', 'sb1', 'sw2', 'sb2')}
    del _L1_ffn_all
    return {'x': x, 'ctx_768': ctx_768, 'mask_BxS2_bk0': mask_BxS2_bk0, 'mask_BxS_bf1': mask_BxS_bf1, 'mask_BxS2_bf1': mask_BxS2_bf1, 'L0_attn_W_qkv': _L0_attn_in['W_qkv'], 'L0_attn_b_qkv': _L0_attn_in['b_qkv'], 'L0_attn_W_out': _L0_attn_in['W_out'], 'L0_attn_b_out': _L0_attn_in['b_out'], 'L0_xattn_ln_x_g': _L0_xattn_in['ln_x_g'], 'L0_xattn_ln_x_b': _L0_xattn_in['ln_x_b'], 'L0_xattn_ln_l_g': _L0_xattn_in['ln_l_g'], 'L0_xattn_ln_l_b': _L0_xattn_in['ln_l_b'], 'L0_xattn_qn_g': _L0_xattn_in['qn_g'], 'L0_xattn_kn_g': _L0_xattn_in['kn_g'], 'L0_xattn_Wq': _L0_xattn_in['Wq'], 'L0_xattn_Wkv': _L0_xattn_in['Wkv'], 'L0_xattn_Wlkv': _L0_xattn_in['Wlkv'], 'L0_xattn_Wo': _L0_xattn_in['Wo'], 'L0_xattn_bo': _L0_xattn_in['bo'], 'L0_ffn_Wr': _L0_ffn_in['Wr'], 'L0_ffn_W1': _L0_ffn_in['W1'], 'L0_ffn_W2': _L0_ffn_in['W2'], 'L1_attn_Wq': _L1_attn_in['Wq'], 'L1_attn_Wk': _L1_attn_in['Wk'], 'L1_attn_Wv': _L1_attn_in['Wv'], 'L1_attn_pre_proj': _L1_attn_in['pre_proj'], 'L1_attn_post_proj': _L1_attn_in['post_proj'], 'L1_attn_mem_k': _L1_attn_in['mem_k'], 'L1_attn_mem_v': _L1_attn_in['mem_v'], 'L1_attn_Wo': _L1_attn_in['Wo'], 'L1_attn_bo': _L1_attn_in['bo'], 'L1_xattn_Wq': _L1_xattn_in['Wq'], 'L1_xattn_Wk': _L1_xattn_in['Wk'], 'L1_xattn_Wv': _L1_xattn_in['Wv'], 'L1_xattn_W_film_in': _L1_xattn_in['W_film_in'], 'L1_xattn_b_film_in': _L1_xattn_in['b_film_in'], 'L1_xattn_W_film_out': _L1_xattn_in['W_film_out'], 'L1_xattn_b_film_out': _L1_xattn_in['b_film_out'], 'L1_xattn_g_norm_in': _L1_xattn_in['g_norm_in'], 'L1_xattn_b_norm_in': _L1_xattn_in['b_norm_in'], 'L1_xattn_g_norm_out': _L1_xattn_in['g_norm_out'], 'L1_xattn_b_norm_out': _L1_xattn_in['b_norm_out'], 'L1_xattn_g_ffn': _L1_xattn_in['g_ffn'], 'L1_xattn_b_ffn': _L1_xattn_in['b_ffn'], 'L1_xattn_W1': _L1_xattn_in['W1'], 'L1_xattn_b1': _L1_xattn_in['b1'], 'L1_xattn_W2': _L1_xattn_in['W2'], 'L1_xattn_b2': _L1_xattn_in['b2'], 'L1_xattn_log_dt': _L1_xattn_in['log_dt'], 'L1_xattn_A_re': _L1_xattn_in['A_re'], 'L1_xattn_A_im': _L1_xattn_in['A_im'], 'L1_xattn_C_re': _L1_xattn_in['C_re'], 'L1_xattn_C_im': _L1_xattn_in['C_im'], 'L1_xattn_D_skip': _L1_xattn_in['D_skip'], 'L1_xattn_mod_gate': _L1_xattn_in['mod_gate'], 'L1_ffn_router_w': _L1_ffn_in['router_w'], 'L1_ffn_router_b': _L1_ffn_in['router_b'], 'L1_ffn_w1': _L1_ffn_in['w1'], 'L1_ffn_b1': _L1_ffn_in['b1'], 'L1_ffn_w2': _L1_ffn_in['w2'], 'L1_ffn_b2': _L1_ffn_in['b2'], 'L1_ffn_sw1': _L1_ffn_in['sw1'], 'L1_ffn_sb1': _L1_ffn_in['sb1'], 'L1_ffn_sw2': _L1_ffn_in['sw2'], 'L1_ffn_sb2': _L1_ffn_in['sb2']}

def reference(x, ctx_768, mask_BxS2_bk0, mask_BxS_bf1, mask_BxS2_bf1, L0_attn_W_qkv, L0_attn_b_qkv, L0_attn_W_out, L0_attn_b_out, L0_xattn_ln_x_g, L0_xattn_ln_x_b, L0_xattn_ln_l_g, L0_xattn_ln_l_b, L0_xattn_qn_g, L0_xattn_kn_g, L0_xattn_Wq, L0_xattn_Wkv, L0_xattn_Wlkv, L0_xattn_Wo, L0_xattn_bo, L0_ffn_Wr, L0_ffn_W1, L0_ffn_W2, L1_attn_Wq, L1_attn_Wk, L1_attn_Wv, L1_attn_pre_proj, L1_attn_post_proj, L1_attn_mem_k, L1_attn_mem_v, L1_attn_Wo, L1_attn_bo, L1_xattn_Wq, L1_xattn_Wk, L1_xattn_Wv, L1_xattn_W_film_in, L1_xattn_b_film_in, L1_xattn_W_film_out, L1_xattn_b_film_out, L1_xattn_g_norm_in, L1_xattn_b_norm_in, L1_xattn_g_norm_out, L1_xattn_b_norm_out, L1_xattn_g_ffn, L1_xattn_b_ffn, L1_xattn_W1, L1_xattn_b1, L1_xattn_W2, L1_xattn_b2, L1_xattn_log_dt, L1_xattn_A_re, L1_xattn_A_im, L1_xattn_C_re, L1_xattn_C_im, L1_xattn_D_skip, L1_xattn_mod_gate, L1_ffn_router_w, L1_ffn_router_b, L1_ffn_w1, L1_ffn_b1, L1_ffn_w2, L1_ffn_b2, L1_ffn_sw1, L1_ffn_sb1, L1_ffn_sw2, L1_ffn_sb2):
    import jax
    import jax.numpy as jnp

    def _L0_attn_ref(x, W_qkv, b_qkv, W_out, b_out):
        import jax, jax.numpy as jnp
        import numpy as np
        D_MODEL = 256
        NUM_HEADS = 16
        D_K = D_MODEL // NUM_HEADS
        B, S, _ = x.shape
        qkv = (jnp.einsum('bsd,de->bse', x, W_qkv) + b_qkv).reshape(B, S, NUM_HEADS, 3 * D_K)
        q, k, v = (qkv[..., :D_K], qkv[..., D_K:2 * D_K], qkv[..., 2 * D_K:])
        scores = jnp.einsum('bshd,bsgd->bshg', q, k) / np.sqrt(D_K)
        attn = jax.nn.softmax(scores, axis=-1)
        context = jnp.einsum('bshg,bsgd->bshd', attn, v).reshape(B, S, NUM_HEADS * D_K)
        return jnp.einsum('bsd,de->bse', context, W_out) + b_out

    def _L0_xattn_ref(x, latents, mask, ln_x_g, ln_x_b, ln_l_g, ln_l_b, qn_g, kn_g, Wq, Wkv, Wlkv, Wo, bo):
        import jax, jax.numpy as jnp
        import numpy as np
        DIM_IN, DIM_LAT, DIM_HEAD = (192, 256, 64)
        INNER = max(DIM_LAT, DIM_IN)
        HEADS = INNER // DIM_HEAD
        SCALE = DIM_HEAD ** (-0.5)
        RMS_EPS = 1e-08
        LN_EPS = 1e-05

        def layernorm(x, g, b):
            mu = jnp.mean(x, axis=-1, keepdims=True)
            var = jnp.mean((x - mu) ** 2, axis=-1, keepdims=True)
            return (x - mu) * jax.lax.rsqrt(var + LN_EPS) * g + b

        def rmsnorm(x, gamma):
            norm = jnp.sqrt(jnp.sum(x * x, axis=-1, keepdims=True)) * x.shape[-1] ** (-0.5)
            return x / jnp.maximum(norm, RMS_EPS) * gamma
        b, n, _ = x.shape
        m = latents.shape[1]
        xn = layernorm(x, ln_x_g, ln_x_b)
        ln = layernorm(latents, ln_l_g, ln_l_b)
        q = ln @ Wq.T
        kv = jnp.concatenate([xn @ Wkv.T, ln @ Wlkv.T], axis=1)
        k, v = (kv[..., :INNER], kv[..., INNER:])
        split_heads = lambda t: t.reshape(t.shape[0], t.shape[1], HEADS, DIM_HEAD).transpose(0, 2, 1, 3)
        q, k, v = (split_heads(q), split_heads(k), split_heads(v))
        qn = rmsnorm(q, qn_g) * SCALE
        kn = rmsnorm(k, kn_g)
        attn = jnp.einsum('bhid,bhjd->bhij', qn, kn)
        full_mask = jnp.pad(mask, ((0, 0), (0, m)), constant_values=True)
        attn = jnp.where(full_mask[:, None, None, :], attn, -jnp.finfo(attn.dtype).max)
        attn = jax.nn.softmax(attn, axis=-1)
        out = jnp.einsum('bhij,bhjd->bhid', attn, v)
        out = out.transpose(0, 2, 1, 3).reshape(b, m, INNER)
        return out @ Wo.T + bo

    def _L0_ffn_ref(h, Wr, W1, W2):
        import jax, jax.numpy as jnp
        import numpy as np
        B, S, H, E, F = (2, 512, 256, 8, 1024)
        g = jax.nn.softmax(h @ Wr, axis=-1)
        top2_w, top2_idx = jax.lax.top_k(g, 2)
        top2_w = top2_w / jnp.sum(top2_w, axis=-1, keepdims=True)
        hid = jax.nn.relu(jnp.einsum('bsh,ehf->bsef', h, W1))
        expert_out = jnp.einsum('bsef,efh->bseh', hid, W2)
        top2_out = jnp.take_along_axis(expert_out, top2_idx[..., None], axis=2)
        return jnp.sum(top2_out * top2_w[..., None], axis=2)

    def _L1_attn_ref(x, Wq, Wk, Wv, pre_proj, post_proj, mem_k, mem_v, Wo, bo):
        import jax, jax.numpy as jnp
        import numpy as np
        from jax import lax
        B, N, DIM = (2, 512, 256)
        HEADS, DHEAD = (16, 64)
        NUM_MEM_KV = 16
        SPARSE_TOPK = 64
        INNER = HEADS * DHEAD
        b, n, _ = x.shape
        h, m, d = mem_k.shape
        scale = d ** (-0.5)

        def split_heads(t):
            return t.reshape(b, n, h, d).transpose(0, 2, 1, 3)
        q = split_heads(x @ Wq)
        k = split_heads(x @ Wk)
        v = split_heads(x @ Wv)
        k = jnp.concatenate([jnp.broadcast_to(mem_k[None], (b, h, m, d)), k], axis=2)
        v = jnp.concatenate([jnp.broadcast_to(mem_v[None], (b, h, m, d)), v], axis=2)
        dots = jnp.einsum('bhid,bhjd->bhij', q, k) * scale
        neg = -jnp.finfo(dots.dtype).max
        dots = jnp.einsum('bhij,hk->bkij', dots, pre_proj)
        j = m + n
        ii = jnp.arange(n)[:, None]
        jj = jnp.arange(j)[None, :]
        causal = jj - m > ii
        dots = jnp.where(causal[None, None], neg, dots)
        top = lax.top_k(dots, SPARSE_TOPK)[0]
        vk = top[..., -1:]
        dots = jnp.where(dots < vk, neg, dots)
        attn = jax.nn.softmax(dots, axis=-1)
        attn = jnp.einsum('bhij,hk->bkij', attn, post_proj)
        out = jnp.einsum('bhij,bhjd->bhid', attn, v)
        out = out.transpose(0, 2, 1, 3).reshape(b, n, h * d)
        return out @ Wo + bo

    def _L1_xattn_ref(x_text, x_vision, text_mask, vision_mask, Wq, Wk, Wv, W_film_in, b_film_in, W_film_out, b_film_out, g_norm_in, b_norm_in, g_norm_out, b_norm_out, g_ffn, b_ffn, W1, b1, W2, b2, log_dt, A_re, A_im, C_re, C_im, D_skip, mod_gate):
        import jax, jax.numpy as jnp
        import numpy as np
        B, T, DT, G, DV = (16, 128, 256, 144, 192)
        H, DH = (4, 32)
        INNER = H * DH
        HID = 4 * DT
        N_STATE = 64
        K_TOP = 32

        def layernorm(x, g, b, eps=1e-05):
            m = x.mean(-1, keepdims=True)
            v = x.var(-1, keepdims=True)
            return (x - m) * jax.lax.rsqrt(v + eps) * g + b

        def s4d(x, log_dt, A_re, A_im, C_re, C_im, D_skip):
            Bb, L, D = x.shape
            dt = jnp.exp(log_dt)
            A = A_re + 1j * A_im
            C = C_re + 1j * C_im
            dtA = dt[:, None] * A
            dC = C * (jnp.exp(dtA) - 1.0) / A
            powers = jnp.exp(dtA[:, :, None] * jnp.arange(L))
            K = 2.0 * jnp.einsum('dn,dnl->dl', dC, powers).real
            n = 2 * L
            Kf = jnp.fft.rfft(K, n=n, axis=-1)
            xf = jnp.fft.rfft(x, n=n, axis=1)
            y = jnp.fft.irfft(xf * Kf.T[None], n=n, axis=1)[:, :L]
            return y + x * D_skip
        Bb, Tt, D = x_text.shape
        Gg = x_vision.shape[1]
        Q = (x_text @ Wq).reshape(Bb, Tt, H, DH)
        K = (x_vision @ Wk).reshape(Bb, Gg, H, DH)
        scores = jnp.einsum('bthd,bghd->bhtg', Q, K) / np.sqrt(DH).astype(np.float32)
        scores = jnp.where(vision_mask[:, None, None, :], scores, -jnp.inf)
        topv, topi = jax.lax.top_k(scores, K_TOP)
        probs = jax.nn.softmax(topv, axis=-1)
        bi = jnp.arange(Bb)[:, None, None, None]
        hi = jnp.arange(H)[None, :, None, None]
        ti = jnp.arange(Tt)[None, None, :, None]
        attn = jnp.zeros_like(scores).at[bi, hi, ti, topi].set(probs)
        attn_mean = attn.mean(axis=1)
        V = x_vision @ Wv
        c_t = jnp.einsum('btg,bgd->btd', attn_mean, V)
        c_t = c_t * text_mask[..., None]
        x = layernorm(x_text, g_norm_in, b_norm_in)
        scale_in, shift_in = jnp.split(c_t @ W_film_in + b_film_in, 2, axis=-1)
        x = x * (1.0 + mod_gate * scale_in) + mod_gate * shift_in
        y = s4d(x, log_dt, A_re, A_im, C_re, C_im, D_skip)
        scale_out, shift_out = jnp.split(c_t @ W_film_out + b_film_out, 2, axis=-1)
        y = y * (1.0 + mod_gate * scale_out) + mod_gate * shift_out
        xt = x_text + y
        h = layernorm(xt, g_ffn, b_ffn)
        h = jax.nn.gelu(h @ W1 + b1, approximate=False) @ W2 + b2
        xt = xt + h
        return layernorm(xt, g_norm_out, b_norm_out)

    def _L1_ffn_ref(x, router_w, router_b, w1, b1, w2, b2, sw1, sb1, sw2, sb2):
        import jax, jax.numpy as jnp
        import numpy as np
        B, S, D = (4, 128, 256)
        E, K, H = (64, 8, 64)
        ES, HS = (2, 512)
        b_, s_, d_ = x.shape
        xf = x.reshape(-1, d_)
        probs = jax.nn.softmax(xf @ router_w + router_b, axis=-1)
        tw, ti = jax.lax.top_k(probs, K)
        tw = tw / jnp.sum(tw, axis=-1, keepdims=True)

        def body(acc, p):
            W1, B1, W2, B2, e = p
            h = jax.nn.silu(xf @ W1 + B1) @ W2 + B2
            cw = jnp.sum(jnp.where(ti == e, tw, 0.0), axis=-1)
            return (acc + cw[:, None] * h, None)
        routed, _ = jax.lax.scan(body, jnp.zeros_like(xf), (w1, b1, w2, b2, jnp.arange(w1.shape[0])))

        def shared_mlp(W1, B1, W2, B2):
            return jax.nn.silu(xf @ W1 + B1) @ W2 + B2
        shared = jnp.sum(jax.vmap(shared_mlp)(sw1, sb1, sw2, sb2), axis=0)
        return (routed + shared).reshape(b_, s_, d_)
    x = _layernorm(x + _L0_attn_ref(x, L0_attn_W_qkv, L0_attn_b_qkv, L0_attn_W_out, L0_attn_b_out), axis=-1)
    x = _layernorm(x + _L0_xattn_ref(ctx_768, x, mask_BxS2_bk0, L0_xattn_ln_x_g, L0_xattn_ln_x_b, L0_xattn_ln_l_g, L0_xattn_ln_l_b, L0_xattn_qn_g, L0_xattn_kn_g, L0_xattn_Wq, L0_xattn_Wkv, L0_xattn_Wlkv, L0_xattn_Wo, L0_xattn_bo), axis=-1)
    x = _layernorm(x + _L0_ffn_ref(x, L0_ffn_Wr, L0_ffn_W1, L0_ffn_W2), axis=-1)
    x = _layernorm(x + _L1_attn_ref(x, L1_attn_Wq, L1_attn_Wk, L1_attn_Wv, L1_attn_pre_proj, L1_attn_post_proj, L1_attn_mem_k, L1_attn_mem_v, L1_attn_Wo, L1_attn_bo), axis=-1)
    x = _layernorm(x + _L1_xattn_ref(x, ctx_768, mask_BxS_bf1, mask_BxS2_bf1, L1_xattn_Wq, L1_xattn_Wk, L1_xattn_Wv, L1_xattn_W_film_in, L1_xattn_b_film_in, L1_xattn_W_film_out, L1_xattn_b_film_out, L1_xattn_g_norm_in, L1_xattn_b_norm_in, L1_xattn_g_norm_out, L1_xattn_b_norm_out, L1_xattn_g_ffn, L1_xattn_b_ffn, L1_xattn_W1, L1_xattn_b1, L1_xattn_W2, L1_xattn_b2, L1_xattn_log_dt, L1_xattn_A_re, L1_xattn_A_im, L1_xattn_C_re, L1_xattn_C_im, L1_xattn_D_skip, L1_xattn_mod_gate), axis=-1)
    x = _layernorm(x + _L1_ffn_ref(x, L1_ffn_router_w, L1_ffn_router_b, L1_ffn_w1, L1_ffn_b1, L1_ffn_w2, L1_ffn_b2, L1_ffn_sw1, L1_ffn_sb1, L1_ffn_sw2, L1_ffn_sb2), axis=-1)
    return x

_drawn_inputs = setup_inputs


def setup_inputs(seed=0):
    import zlib

    import numpy as np

    out = dict(_drawn_inputs(seed))
    spreads = {'L0_xattn_ln_x_g': (1.0, 0.569),
     'L0_xattn_ln_x_b': (0.0, 0.321),
     'L0_xattn_ln_l_g': (1.0, 0.2),
     'L0_xattn_ln_l_b': (0.0, 0.1),
     'L0_xattn_qn_g': (1.0, 0.2),
     'L0_xattn_kn_g': (1.0, 0.2),
     'L0_xattn_bo': (0.0, 0.1),
     'L1_attn_bo': (0.0, 0.1),
     'L1_xattn_b_film_in': (0.0, 0.1),
     'L1_xattn_b_film_out': (0.0, 0.289),
     'L1_xattn_g_norm_in': (1.0, 0.2),
     'L1_xattn_b_norm_in': (0.0, 0.1),
     'L1_xattn_g_norm_out': (1.0, 0.2),
     'L1_xattn_b_norm_out': (0.0, 0.1),
     'L1_xattn_g_ffn': (1.0, 0.6),
     'L1_xattn_b_ffn': (0.0, 0.8),
     'L1_xattn_b1': (0.0, 0.701),
     'L1_xattn_b2': (0.0, 0.1),
     'L1_xattn_A_re': (-0.5, 0.2),
     'L1_ffn_router_b': (0.0, 0.359),
     'L1_ffn_b1': (0.0, 0.8),
     'L1_ffn_b2': (0.0, 0.1),
     'L1_ffn_sb1': (0.0, 0.276),
     'L1_ffn_sb2': (0.0, 0.1)}
    factors = {'L1_xattn_Wq': 8.0,
     'L1_xattn_Wk': 8.0,
     'L1_xattn_W_film_in': 3.181,
     'L1_xattn_W_film_out': 4.429,
     'L1_ffn_w1': 6.147,
     'L1_ffn_w2': 5.838}
    for name, (base, spread) in spreads.items():
        noise = np.random.default_rng([zlib.crc32(name.encode()), seed]).standard_normal(out[name].shape)
        drawn = base * np.exp(spread * noise) if base else spread * noise
        out[name] = jnp.asarray(drawn.astype(out[name].dtype))
    for name, factor in factors.items():
        out[name] = (out[name] * factor).astype(out[name].dtype)
    return out
```

```python
from contextlib import ExitStack

import numpy as np
import concourse.bass as bass
from concourse import mybir

F32 = mybir.dt.float32
I32 = mybir.dt.int32
U8 = mybir.dt.uint8
ACT = mybir.ActivationFunctionType
ALU = mybir.AluOpType
AX = mybir.AxisListType

P = 128
B, S, D = 4, 512, 256
NT = S // P
TT = B * NT
KD = D // P
EPS = 1e-5


class Shared:

    def __init__(self, nc, ctx, dram):
        self.nc, self.dram = nc, dram

        def sb(name, shape):
            return ctx.enter_context(nc.sbuf_tensor(name, shape, F32))

        self.x = sb("x", [P, TT, D])
        self.branch = sb("branch", [P, TT, D])
        self.xT = sb("xT", [P, KD, B * S])
        self.ident = sb("ident", [P, P])
        self.ctxT = ctx.enter_context(nc.sbuf_tensor("ctxT", [PC, 2, B * C], F32))


def buffers(nc, ctx, tag):
    def sb(name, shape, dt=F32):
        return ctx.enter_context(nc.sbuf_tensor(f"{tag}_{name}", shape, dt))

    def ps(name, shape):
        return ctx.enter_context(nc.psum_tensor(f"{tag}_{name}", shape, F32))

    def sem(name):
        return ctx.enter_context(nc.semaphore(f"{tag}_{name}"))

    return sb, ps, sem


def turn_semaphores(nc, ctx, tag):
    taken = []

    def sem(name):
        taken.append(ctx.enter_context(nc.semaphore(f"{tag}_{name}")))
        return taken[-1]

    def clear():
        for x in taken:
            nc.sync.sem_clear(x)
        nc.all_engine_barrier()

    return sem, clear


def recycle(nc):
    free = sorted(nc.released_uncleared_semaphores)
    while free:
        n = 1
        while n < len(free) and free[n] == free[0] + n:
            n += 1
        nc.sync.sem_clear(range(free[0], free[0] + n))
        free = free[n:]
    nc.all_engine_barrier()


def load_inputs(nc, G):
    with ExitStack() as ctx:
        sb, ps, sem = buffers(nc, ctx, "ld")
        loaded = sem("loaded")
        with nc.Block() as block:
            @block.sync
            def _(sp):
                sp.dma_start(G.ident[:], G.dram["c_ident"]).then_inc(loaded, 16)
                for b in range(B):
                    sp.dma_start(G.x[:, b * NT:(b + 1) * NT, :],
                                 G.dram["x"][b].rearrange("(t p) d -> p t d", p=P)).then_inc(loaded, 16)
                sp.wait_ge(loaded, 16 * (B + 1))


def chain(eng, sem):
    count = [0]

    def step(ins):
        count[0] += 1
        ins.then_inc(sem, 1)
        eng.wait_ge(sem, count[0])

    return step


def norm_stage(nc, G, tag, add=True, norm=True, turn=True, store=None, src=None, dst=None, gain=None):
    src = G.x if src is None else src
    dst = G.x if dst is None else dst
    with ExitStack() as ctx:
        sb, ps, sem = buffers(nc, ctx, tag)
        stats = sb("stats", [P, TT, 6])
        mv = sb("mv", [P, TT, 2])
        std = sb("std", [P, TT])
        rstd = sb("rstd", [P, TT])
        gb = sb("gb", [P, 2, KD])
        pT = [ps(f"pT{i}", [P, NT, P]) for i in range(2)]
        moments_ready, std_ready, x_ready = sem("moments_ready"), sem("std_ready"), sem("x_ready")
        turned, copied, dve_steps, stored = sem("turned"), sem("copied"), sem("dve_steps"), sem("stored")
        loaded = sem("loaded")
        sums = B if add else 0
        with nc.Block() as block:
            if gain is not None:
                @block.sync
                def _(sp):
                    with nc.allow_non_contiguous_dma(reason="a gain's features onto partitions"):
                        for i, v in enumerate(gain):
                            sp.dma_start(gb[:, i, :], v.rearrange("(k p) -> p k", p=P)).then_inc(loaded, 16)

            if norm:
                @block.vector
                def _(dve):
                    step = chain(dve, dve_steps)
                    if add:
                        for t in range(0, TT, NT):
                            dve.tensor_tensor(G.x[:, t:t + NT, :], G.x[:, t:t + NT, :],
                                              G.branch[:, t:t + NT, :], ALU.add).then_inc(x_ready, 1)
                    for t in range(TT):
                        if add and t % NT == 0:
                            dve.wait_ge(x_ready, t // NT + 1)
                        ins = dve.bn_stats(stats[:, t, :], src[:, t, :])
                    step(ins)
                    for t in range(TT):
                        ins = dve.bn_aggr(mv[:, t, :], stats[:, t, :])
                    step(ins)
                    dve.tensor_scalar(rstd[:], mv[:, :, 1], EPS, None, ALU.add).then_inc(moments_ready, 1)
                    dve.wait_ge(std_ready, 1)
                    step(dve.reciprocal(rstd[:], std[:]))
                    for t in range(TT):
                        dve.tensor_scalar(dst[:, t, :], src[:, t, :], mv[:, t, 0:1], rstd[:, t:t + 1],
                                          ALU.subtract, ALU.mult).then_inc(x_ready, 1)

            @block.scalar
            def _(act):
                if norm:
                    act.wait_ge(moments_ready, 1)
                    act.activation(std[:], rstd[:], ACT.Sqrt).then_inc(std_ready, 1)
                if store is None and turn:
                    if gain is not None:
                        act.wait_ge(loaded, 32)
                    for n in range(B * KD):
                        b, k = n // KD, n % KD
                        act.wait_ge(turned, n + 1)
                        to, turned_tile = G.xT[:, k, b * S:(b + 1) * S], pT[n % 2][:].rearrange("p a b -> p (a b)")
                        if gain is None:
                            act.copy(to, turned_tile).then_inc(copied, 1)
                        else:
                            act.activation(to, turned_tile, ACT.Identity, bias=gb[:, 1, k:k + 1],
                                           scale=gb[:, 0, k:k + 1]).then_inc(copied, 1)

            if store is None and turn:
                @block.tensor
                def _(pe):
                    for n in range(B * KD):
                        b, k = n // KD, n % KD
                        if norm:
                            pe.wait_ge(x_ready, sums + (b + 1) * NT)
                        if n >= 2:
                            pe.wait_ge(copied, n - 1)
                        for q in range(NT):
                            ins = pe.transpose(pT[n % 2][:, q, :], dst[:, b * NT + q, k * P:(k + 1) * P],
                                               G.ident[:])
                        ins.then_inc(turned, 1)

            if store is not None:
                @block.sync
                def _(sp):
                    for b in range(B):
                        sp.wait_ge(x_ready, sums + (b + 1) * NT)
                        sp.dma_start(store[b].rearrange("(t p) d -> p t d", p=P),
                                     dst[:, b * NT:(b + 1) * NT, :]).then_inc(stored, 16)
                    sp.wait_ge(stored, 16 * B)


H0, DK0 = 16, 16
POOL_HEADS = 11


def l0_attention(nc, G):
    with ExitStack() as ctx:
        sb, ps, sem = buffers(nc, ctx, "a0")
        w = sb("w", [P, KD, 3 * D])
        wo = sb("wo", [P, KD, D])
        bias = sb("bias", [1, 3 * D])
        bo = sb("bo", [1, D])
        ones = sb("ones", [1, P])
        qkv = sb("qkv", [P, 3, H0, 3 * DK0])
        prod = sb("prod", [P, 2, H0, H0, DK0])
        mixed = sb("mixed", [P, 2, H0, DK0, H0])
        score = sb("score", [P, 2, H0, H0])
        probs = sb("probs", [P, 2, H0, H0])
        top = sb("top", [P, H0])
        den = sb("den", [P, H0])
        cx = sb("cx", [P, 2, D])
        cT = sb("cT", [P, 2, KD, P])
        pq = [ps(f"pq{i}", [P, 2, 512]) for i in range(2)]
        pc = [ps(f"pc{i}", [P, KD, P]) for i in range(2)]
        py = [ps(f"py{i}", [P, D]) for i in range(2)]
        loaded = sem("loaded")
        qkv_full, qkv_ready, prod_ready, score_ready = sem("qkv_full"), sem("qkv_ready"), sem("prod_ready"), sem("score_ready")
        exp_ready, probs_ready, mixed_ready, cx_ready = sem("exp_ready"), sem("probs_ready"), sem("mixed_ready"), sem("cx_ready")
        turned, cT_ready, y_full, y_done, dve_steps = sem("turned"), sem("cT_ready"), sem("y_full"), sem("y_done"), sem("dve_steps")
        one = sem("one")
        d = G.dram

        with nc.Block() as block:
            @block.sync
            def _(sp):
                sp.dma_start(w[:], d["L0_attn_W_qkv"].rearrange("(k p) n -> p k n", p=P)).then_inc(loaded, 16)
                sp.dma_start(bias[:], d["L0_attn_b_qkv"].rearrange("(a n) -> a n", a=1)).then_inc(loaded, 16)
                sp.dma_start(wo[:], d["L0_attn_W_out"].rearrange("(k p) n -> p k n", p=P)).then_inc(loaded, 16)
                sp.dma_start(bo[:], d["L0_attn_b_out"].rearrange("(a n) -> a n", a=1)).then_inc(loaded, 16)

            @block.tensor
            def _(pe):
                pe.wait_ge(loaded, 64)
                pe.wait_ge(one, 1)

                def project(i):
                    if i >= 2:
                        pe.wait_ge(qkv_ready, i - 1)
                    for c, (lo, hi) in enumerate(((0, 512), (512, 768))):
                        for k in range(KD):
                            pe.matmul(pq[i % 2][:, c, 0:hi - lo], G.xT[:, k, i * P:(i + 1) * P],
                                      w[:, k, lo:hi], start=(k == 0), stop=False)
                        ins = pe.matmul(pq[i % 2][:, c, 0:hi - lo], ones[:], bias[:, lo:hi], start=False, stop=True)
                    ins.then_inc(qkv_full, 1)

                def turn(i):
                    pe.wait_ge(cx_ready, i + 1)
                    if i >= 2:
                        pe.wait_ge(cT_ready, i - 1)
                    for k in range(KD):
                        ins = pe.transpose(pc[i % 2][:, k, :], cx[:, i % 2, k * P:(k + 1) * P], G.ident[:])
                    ins.then_inc(turned, 1)

                def out(i):
                    pe.wait_ge(cT_ready, i + 1)
                    if i >= 2:
                        pe.wait_ge(y_done, i - 1)
                    for k in range(KD):
                        pe.matmul(py[i % 2][:], cT[:, i % 2, k, :], wo[:, k, :], start=(k == 0), stop=False)
                    pe.matmul(py[i % 2][:], ones[:], bo[:], start=False, stop=True).then_inc(y_full, 1)

                project(0)
                project(1)
                for i in range(TT):
                    if i + 2 < TT:
                        project(i + 2)
                    if i >= 3:
                        turn(i - 3)
                        out(i - 3)
                for i in range(TT - 3, TT):
                    turn(i)
                    out(i)

            def product(eng, i, lo, hi):
                shape = [P, hi - lo, H0, DK0]
                q = qkv[:, i % 3, lo:hi, 0:16].unsqueeze(2).to_broadcast(shape)
                k = qkv[:, i % 3, :, 16:32].unsqueeze(1).to_broadcast(shape)
                return eng.tensor_tensor(prod[:, i % 2, lo:hi], q, k, ALU.mult)

            def weighing(eng, i, lo, hi):
                shape = [P, hi - lo, DK0, H0]
                p = probs[:, i % 2, lo:hi].unsqueeze(2).to_broadcast(shape)
                v = qkv[:, i % 3, :, 32:48].rearrange("p g c -> p c g").unsqueeze(1).to_broadcast(shape)
                return eng.tensor_tensor(mixed[:, i % 2, lo:hi], p, v, ALU.mult)

            @block.gpsimd
            def _(pool):
                for i in range(TT + 1):
                    if i < TT:
                        pool.wait_ge(qkv_ready, i + 1)
                        if i >= 2:
                            pool.wait_ge(score_ready, i - 1)
                        product(pool, i, 0, POOL_HEADS).then_inc(prod_ready, 1)
                    if i >= 1:
                        j = i - 1
                        pool.wait_ge(probs_ready, j + 1)
                        if j >= 2:
                            pool.wait_ge(cx_ready, j - 1)
                        weighing(pool, j, 0, POOL_HEADS).then_inc(mixed_ready, 1)

            @block.scalar
            def _(act):
                def evacuate(i):
                    act.wait_ge(qkv_full, i + 1)
                    if i >= 3:
                        act.wait_ge(cx_ready, i - 2)
                    flat = qkv[:, i % 3].rearrange("p h c -> p (h c)")
                    act.copy(flat[:, 0:512], pq[i % 2][:, 0, :])
                    act.copy(flat[:, 512:768], pq[i % 2][:, 1, 0:256]).then_inc(qkv_ready, 1)

                evacuate(0)
                evacuate(1)
                evacuate(2)
                for i in range(TT + 4):
                    if i < TT:
                        act.wait_ge(score_ready, i + 1)
                        if i >= 2:
                            act.wait_ge(cx_ready, i - 1)
                        act.activation(probs[:, i % 2], score[:, i % 2], ACT.Exp, scale=DK0 ** -0.5
                                       ).then_inc(exp_ready, 1)
                    if 1 <= i and i + 2 < TT:
                        evacuate(i + 2)
                    if 3 <= i < TT + 3:
                        j = i - 3
                        act.wait_ge(turned, j + 1)
                        if j >= 2:
                            act.wait_ge(y_full, j - 1)
                        act.copy(cT[:, j % 2], pc[j % 2][:]).then_inc(cT_ready, 1)
                    if i >= 4:
                        j = i - 4
                        act.wait_ge(y_full, j + 1)
                        act.copy(G.branch[:, j, :], py[j % 2][:]).then_inc(y_done, 1)

            @block.vector
            def _(dve):
                step = chain(dve, dve_steps)
                dve.memset(ones[:], 1.0).then_inc(one, 1)

                def scores(i):
                    dve.wait_ge(qkv_ready, i + 1)
                    step(product(dve, i, POOL_HEADS, H0))
                    if i >= 2:
                        dve.wait_ge(exp_ready, i - 1)
                    dve.reduce_sum(score[:, i % 2, POOL_HEADS:], prod[:, i % 2, POOL_HEADS:], AX.X)
                    dve.wait_ge(prod_ready, i + 1)
                    step(dve.reduce_sum(score[:, i % 2, 0:POOL_HEADS], prod[:, i % 2, 0:POOL_HEADS], AX.X))
                    step(dve.reduce_max(top[:], score[:, i % 2], AX.X))
                    dve.tensor_tensor(score[:, i % 2], score[:, i % 2],
                                      top[:].unsqueeze(2).to_broadcast([P, H0, H0]), ALU.subtract
                                      ).then_inc(score_ready, 1)

                def normalise(i):
                    dve.wait_ge(exp_ready, i + 1)
                    step(dve.reduce_sum(den[:], probs[:, i % 2], AX.X))
                    step(dve.reciprocal(den[:], den[:]))
                    dve.tensor_tensor(probs[:, i % 2], probs[:, i % 2],
                                      den[:].unsqueeze(2).to_broadcast([P, H0, H0]), ALU.mult
                                      ).then_inc(probs_ready, 1)

                def contexts(i):
                    dve.wait_ge(probs_ready, i + 1)
                    step(weighing(dve, i, POOL_HEADS, H0))
                    if i >= 2:
                        dve.wait_ge(turned, i - 1)
                    c = cx[:, i % 2].rearrange("p (h c) -> p h c", h=H0)
                    step(dve.reduce_sum(c[:, POOL_HEADS:], mixed[:, i % 2, POOL_HEADS:], AX.X))
                    dve.wait_ge(mixed_ready, i + 1)
                    dve.reduce_sum(c[:, 0:POOL_HEADS], mixed[:, i % 2, 0:POOL_HEADS], AX.X).then_inc(cx_ready, 1)

                for i in range(TT + 1):
                    if i < TT:
                        scores(i)
                    if i >= 1:
                        contexts(i - 1)
                    if i < TT:
                        normalise(i)


C, DC = 64, 192
PC = DC // 2


def context_stage(nc, G):
    with ExitStack() as ctx:
        sb, ps, sem = buffers(nc, ctx, "cx")
        raw = sb("raw", [C, B, DC])
        nrm = sb("nrm", [C, B, DC])
        stats = sb("stats", [C, B, 6])
        mv = sb("mv", [C, B, 2])
        std = sb("std", [C, B])
        gb = sb("gb", [PC, 2, 2])
        pT = [ps(f"pT{i}", [PC, 2, B, C]) for i in range(2)]
        loaded, moments, rooted, normed, turned, dve_steps = (
            sem("loaded"), sem("moments"), sem("rooted"), sem("normed"), sem("turned"), sem("dve_steps"))
        d = G.dram
        with nc.Block() as block:
            @block.sync
            def _(sp):
                sp.dma_start(raw[:], d["ctx_768"].rearrange("b c d -> c b d")).then_inc(loaded, 16)
                with nc.allow_non_contiguous_dma(reason="a gain's features onto partitions"):
                    sp.dma_start(gb[:, 0, :], d["L0_xattn_ln_x_g"].rearrange("(k p) -> p k", p=PC)).then_inc(loaded, 16)
                    sp.dma_start(gb[:, 1, :], d["L0_xattn_ln_x_b"].rearrange("(k p) -> p k", p=PC)).then_inc(loaded, 16)

            @block.vector
            def _(dve):
                step = chain(dve, dve_steps)
                dve.wait_ge(loaded, 48)
                for b in range(B):
                    ins = dve.bn_stats(stats[:, b, :], raw[:, b, :])
                step(ins)
                for b in range(B):
                    ins = dve.bn_aggr(mv[:, b, :], stats[:, b, :])
                step(ins)
                dve.tensor_scalar(std[:], mv[:, :, 1], EPS, None, ALU.add).then_inc(moments, 1)
                dve.wait_ge(rooted, 1)
                step(dve.reciprocal(std[:], std[:]))
                for b in range(B):
                    ins = dve.tensor_scalar(nrm[:, b, :], raw[:, b, :], mv[:, b, 0:1], std[:, b:b + 1],
                                            ALU.subtract, ALU.mult)
                ins.then_inc(normed, 1)

            @block.scalar
            def _(act):
                act.wait_ge(moments, 1)
                act.activation(std[:], std[:], ACT.Sqrt).then_inc(rooted, 1)
                act.wait_ge(turned, 1)
                act.copy(G.ctxT[:], pT[0][:].rearrange("p k b c -> p k (b c)"))
                act.wait_ge(turned, 2)
                for k in range(2):
                    act.activation(G.ctxnT[:, k, :], pT[1][:, k].rearrange("p b c -> p (b c)"), ACT.Identity,
                                   bias=gb[:, 1, k:k + 1], scale=gb[:, 0, k:k + 1])

            @block.tensor
            def _(pe):
                pe.wait_ge(loaded, 48)
                for i, src in enumerate((raw, nrm)):
                    if i == 1:
                        pe.wait_ge(normed, 1)
                    for k in range(2):
                        for b in range(B):
                            ins = pe.transpose(pT[i][:, k, b, :], src[:, b, k * PC:(k + 1) * PC], G.ident[0:C, 0:C])
                    ins.then_inc(turned, 1)


HX, DX = 4, 64
KEYS = S + C


def l0_cross_attention(nc, G):
    with ExitStack() as outer:
        sbo, _, _ = buffers(nc, outer, "x0o")
        qT = sbo("qT", [P, 2, B * S])
        kT = sbo("kT", [P, 2, B, KEYS])
        v = sbo("v", [P, TT, D])
        vc = sbo("vc", [C, B, D])
        cross_project(nc, G, qT, kT, v, vc)
        cross_attend(nc, G, qT, kT, v, vc)


def cross_project(nc, G, qT, kT, v, vc):
    with ExitStack() as ctx:
        sb, ps, sem = buffers(nc, ctx, "xp")
        wq = sb("wq", [P, KD, D])
        wl = sb("wl", [P, KD, 2 * D])
        wc = sb("wc", [PC, 2, 2 * D])
        gain = sb("gain", [P, 2, DX])
        qk = sb("qk", [P, 2, 2 * HX, DX])
        sq = sb("sq", [P, 2, 2 * HX, DX])
        ss = sb("ss", [P, 2, 2 * HX])
        rms = sb("rms", [P, 2, 2 * HX])
        pq = [ps(f"pq{i}", [P, 2, 512]) for i in range(2)]
        pT = [ps(f"pT{i}", [P, 4, P]) for i in range(2)]
        loaded, full, copied, squared, summed = sem("loaded"), sem("full"), sem("copied"), sem("squared"), sem("summed")
        rooted, scaled, gained, turned, stored, dve_steps = (
            sem("rooted"), sem("scaled"), sem("gained"), sem("turned"), sem("stored"), sem("dve_steps"))
        vcopied = sem("vcopied")
        d = G.dram
        N = TT + B

        def part(i):
            return (P, 0) if i < TT else (C, HX)

        with nc.Block() as block:
            @block.sync
            def _(sp):
                sp.dma_start(wq[:], d["L0_xattn_WqT"].rearrange("(k p) n -> p k n", p=P)).then_inc(loaded, 16)
                sp.dma_start(wl[:], d["L0_xattn_WlkvT"].rearrange("(k p) n -> p k n", p=P)).then_inc(loaded, 16)
                sp.dma_start(wc[:], d["L0_xattn_WkvT"].rearrange("(k p) n -> p k n", p=PC)).then_inc(loaded, 16)
                sp.dma_start(gain[:, 0, :], d["L0_xattn_qn_g"].partition_broadcast(P)).then_inc(loaded, 16)
                sp.dma_start(gain[:, 1, :], d["L0_xattn_kn_g"].partition_broadcast(P)).then_inc(loaded, 16)

            @block.tensor
            def _(pe):
                pe.wait_ge(loaded, 80)

                def project(i):
                    if i >= 2:
                        pe.wait_ge(copied, i - 1)
                        pe.wait_ge(vcopied, i - 1)
                    out = pq[i % 2]
                    if i < TT:
                        tokens, w = G.xT[:, :, i * P:(i + 1) * P], wl
                        for k in range(2):
                            pe.matmul(out[:, 0, 0:D], tokens[:, k], wq[:, k, :], start=(k == 0), stop=(k == 1))
                    else:
                        tokens, w = G.ctxnT[:, :, (i - TT) * C:(i - TT + 1) * C], wc
                    n, _ = part(i)
                    for bank, lo, cols in ((0, D, slice(0, D)), (1, 0, slice(D, 2 * D))):
                        for k in range(2):
                            ins = pe.matmul(out[0:n, bank, lo:lo + D], tokens[:, k], w[:, k, cols],
                                            start=(k == 0), stop=(k == 1))
                    ins.then_inc(full, 1)

                def turn(i):
                    n, h0 = part(i)
                    pe.wait_ge(gained, i + 1)
                    if i >= 2:
                        pe.wait_ge(stored, i - 1)
                    for c in range(h0 // 2, 4):
                        ins = pe.transpose(pT[i % 2][:, c, 0:n],
                                           qk[0:n, i % 2, 2 * c:2 * c + 2, :].rearrange("p h c -> p (h c)"),
                                           G.ident[0:n, 0:n])
                    ins.then_inc(turned, 1)

                project(0)
                for i in range(N):
                    if i + 1 < N:
                        project(i + 1)
                    turn(i)

            @block.gpsimd
            def _(pool):
                pool.wait_ge(loaded, 80)

                def square(i):
                    n, h0 = part(i)
                    pool.wait_ge(copied, i + 1)
                    if i >= 2:
                        pool.wait_ge(summed, i - 1)
                    pool.tensor_tensor(sq[0:n, i % 2, h0:8], qk[0:n, i % 2, h0:8], qk[0:n, i % 2, h0:8],
                                       ALU.mult).then_inc(squared, 1)

                for i in range(N):
                    square(i)

            @block.scalar
            def _(act):
                def store(i):
                    n, h0 = part(i)
                    act.wait_ge(turned, i + 1)
                    if i < TT:
                        b, j = i // NT, i % NT
                        act.copy(qT[:, :, i * P:(i + 1) * P], pT[i % 2][:, 0:2, :])
                        act.copy(kT[:, :, b, j * P:(j + 1) * P], pT[i % 2][:, 2:4, :]).then_inc(stored, 1)
                    else:
                        act.copy(kT[:, :, i - TT, S:KEYS], pT[i % 2][:, 2:4, 0:C]).then_inc(stored, 1)

                for i in range(N + 1):
                    if i < N:
                        n, h0 = part(i)
                        act.wait_ge(full, i + 1)
                        to = v[:, i, :] if i < TT else vc[:, i - TT, :]
                        act.copy(to, pq[i % 2][0:n, 1, 0:D]).then_inc(vcopied, 1)
                        act.wait_ge(summed, i + 1)
                        if i >= 2:
                            act.wait_ge(scaled, i - 1)
                        act.activation(rms[0:n, i % 2, h0:8], ss[0:n, i % 2, h0:8], ACT.Sqrt, scale=1.0 / DX
                                       ).then_inc(rooted, 1)
                    if i >= 1:
                        store(i - 1)

            @block.vector
            def _(dve):
                step = chain(dve, dve_steps)
                dve.wait_ge(loaded, 80)

                def copy(i):
                    n, h0 = part(i)
                    dve.wait_ge(full, i + 1)
                    if i >= 2:
                        dve.wait_ge(turned, i - 1)
                    if i < TT:
                        dve.tensor_copy(qk[:, i % 2, 0:HX, :].rearrange("p h c -> p (h c)"), pq[i % 2][:, 0, 0:D])
                    dve.tensor_copy(qk[0:n, i % 2, HX:2 * HX, :].rearrange("p h c -> p (h c)"),
                                    pq[i % 2][0:n, 0, D:2 * D]).then_inc(copied, 1)

                def total(i):
                    n, h0 = part(i)
                    dve.wait_ge(squared, i + 1)
                    if i >= 2:
                        dve.wait_ge(rooted, i - 1)
                    dve.reduce_sum(ss[0:n, i % 2, h0:8], sq[0:n, i % 2, h0:8, :], AX.X).then_inc(summed, 1)

                def scale(i):
                    n, h0 = part(i)
                    dve.wait_ge(rooted, i + 1)
                    r = rms[0:n, i % 2, h0:8]
                    step(dve.tensor_scalar(r, r, 1e-8, None, ALU.max))
                    step(dve.reciprocal(r, r))
                    a = qk[0:n, i % 2, h0:8, :]
                    dve.tensor_tensor(a, a, r.unsqueeze(2).to_broadcast([n, 8 - h0, DX]), ALU.mult).then_inc(scaled, 1)
                    dve.wait_ge(scaled, i + 1)
                    for w, h in ((0, 0), (1, HX)):
                        if h >= h0:
                            a = qk[0:n, i % 2, h:h + HX, :]
                            ins = dve.tensor_tensor(a, a, gain[0:n, w].unsqueeze(1).to_broadcast([n, HX, DX]), ALU.mult)
                    ins.then_inc(gained, 1)

                copy(0)
                for i in range(N):
                    if i + 1 < N:
                        copy(i + 1)
                    total(i)
                    scale(i)


def cross_attend(nc, G, qT, kT, v, vc):
    with ExitStack() as ctx:
        sb, ps, sem = buffers(nc, ctx, "xa")
        wo = sb("wo", [P, KD, D])
        bo = sb("bo", [P, D])
        mask = sb("mask", [1, B * C], U8)
        hide = sb("hide", [1, B * C])
        ones = sb("ones", [1, P])
        probs = sb("probs", [P, 2, KEYS])
        pT_sb = sb("pT_sb", [P, 2, NT + 1, P])
        negmax = sb("negmax", [P, 2])
        den = sb("den", [P, 4])
        rden = sb("rden", [P, 2])
        cx = sb("cx", [P, 2, HX, DX])
        cT = sb("cT", [P, KD, P])
        sc = [ps(f"sc{i}", [P, 1024]) for i in range(2)]
        pT = ps("pT", [P, 8, P])
        pv = ps("pv", [P, 2, HX, DX])
        misc = ps("misc", [P, 512])
        loaded, hidden, scored, maxed, exped = sem("loaded"), sem("hidden"), sem("scored"), sem("maxed"), sem("exped")
        turned, pcopied, weighed, cx_ready = sem("turned"), sem("pcopied"), sem("weighed"), sem("cx_ready")
        cturned, cT_ready, y_full, y_done, dve_steps = (
            sem("cturned"), sem("cT_ready"), sem("y_full"), sem("y_done"), sem("dve_steps"))
        d = G.dram
        scale = DX ** -0.5
        N = TT * HX

        with nc.Block() as block:
            @block.sync
            def _(sp):
                sp.dma_start(wo[:], d["L0_xattn_WoT"].rearrange("(k p) n -> p k n", p=P)).then_inc(loaded, 16)
                sp.dma_start(bo[:], d["L0_xattn_bo"].partition_broadcast(P)).then_inc(loaded, 16)
                sp.dma_start(mask[:], d["mask_BxS2_bk0"].rearrange("(a b) c -> a (b c)", a=1)).then_inc(loaded, 16)

            @block.tensor
            def _(pe):
                pe.wait_ge(loaded, 48)
                pe.wait_ge(hidden, 3)

                def scores(u):
                    i, h = u // HX, u % HX
                    b, r, c = i // NT, slice(64 * (h % 2), 64 * (h % 2) + 64), h // 2
                    if u >= 2:
                        pe.wait_ge(exped, u - 1)
                    q = qT[r, c, i * P:(i + 1) * P]
                    out = sc[u % 2]
                    pe.matmul(out[:, 0:S], q, kT[r, c, b, 0:S], start=True, stop=True)
                    pe.matmul(out[:, S:KEYS], q, kT[r, c, b, S:KEYS], start=True, stop=False)
                    pe.matmul(out[:, S:KEYS], ones[:], hide[:, b * C:(b + 1) * C], start=False, stop=True
                              ).then_inc(scored, 1)

                def turn(u):
                    pe.wait_ge(exped, u + 1)
                    if u >= 1:
                        pe.wait_ge(pcopied, u)
                    for j in range(NT + 1):
                        n = P if j < NT else C
                        ins = pe.transpose(pT[0:n, j, :], probs[:, u % 2, j * P:j * P + n], G.ident[:])
                    ins.then_inc(turned, 1)

                def weigh(u):
                    i, h = u // HX, u % HX
                    b = i // NT
                    pe.wait_ge(pcopied, u + 1)
                    if u >= 1:
                        pe.wait_ge(cx_ready, u)
                    for j in range(NT + 1):
                        n = P if j < NT else C
                        rhs = v[:, b * NT + j, h * DX:(h + 1) * DX] if j < NT else vc[:, b, h * DX:(h + 1) * DX]
                        ins = pe.matmul(pv[:, i % 2, h, :], pT_sb[0:n, u % 2, j, :], rhs,
                                        start=(j == 0), stop=(j == NT))
                    ins.then_inc(weighed, 1)

                def finish(i):
                    pe.wait_ge(cx_ready, HX * (i + 1))
                    if i >= 1:
                        pe.wait_ge(y_done, i)
                    for k in range(KD):
                        ins = pe.transpose(misc[:, k * P:(k + 1) * P],
                                           cx[:, i % 2, 2 * k:2 * k + 2, :].rearrange("p h c -> p (h c)"), G.ident[:])
                    ins.then_inc(cturned, 1)
                    pe.wait_ge(cT_ready, i + 1)
                    for k in range(KD):
                        ins = pe.matmul(misc[:, D:2 * D], cT[:, k, :], wo[:, k, :], start=(k == 0), stop=(k == KD - 1))
                    ins.then_inc(y_full, 1)

                for u in range(N + 4):
                    if u < N:
                        scores(u)
                    if 1 <= u <= N:
                        turn(u - 1)
                    if 2 <= u <= N + 1:
                        weigh(u - 2)
                    if u >= 4 and u % HX == 3 and u // HX >= 1:
                        finish(u // HX - 1)

            @block.scalar
            def _(act):
                for u in range(N + 1):
                    if u < N:
                        act.wait_ge(maxed, u + 1)
                        if u >= 2:
                            act.wait_ge(turned, u - 1)
                        if u >= 4:
                            act.wait_ge(cx_ready, u - 3)
                        act.activation(probs[:, u % 2, :], sc[u % 2][:, 0:KEYS], ACT.Exp, bias=negmax[:, u % 2:u % 2 + 1],
                                       scale=scale, accum_out=den[:, u % 4:u % 4 + 1]).then_inc(exped, 1)
                    if u >= 1:
                        j = u - 1
                        act.wait_ge(turned, j + 1)
                        if j >= 2:
                            act.wait_ge(weighed, j - 1)
                        act.copy(pT_sb[:, j % 2, 0:NT, :], pT[:, 0:NT, :])
                        act.copy(pT_sb[0:C, j % 2, NT, :], pT[0:C, NT, :]).then_inc(pcopied, 1)

            @block.vector
            def _(dve):
                step = chain(dve, dve_steps)
                dve.wait_ge(loaded, 48)
                dve.memset(ones[:], 1.0).then_inc(hidden, 1)
                dve.tensor_copy(hide[:], mask[:]).then_inc(hidden, 1)
                dve.wait_ge(hidden, 2)
                dve.tensor_scalar(hide[:], hide[:], 1.0, 1e30, ALU.subtract, ALU.mult).then_inc(hidden, 1)

                def maximum(u):
                    dve.wait_ge(scored, u + 1)
                    if u >= 2:
                        dve.wait_ge(exped, u - 1)
                    m = negmax[:, u % 2:u % 2 + 1]
                    step(dve.reduce_max(m, sc[u % 2][:, 0:KEYS], AX.X))
                    dve.tensor_scalar(m, m, -scale, None, ALU.mult).then_inc(maxed, 1)

                def normalise(u):
                    i, h = u // HX, u % HX
                    dve.wait_ge(weighed, u + 1)
                    if i >= 2:
                        dve.wait_ge(cturned, i - 1)
                    step(dve.reciprocal(rden[:, u % 2:u % 2 + 1], den[:, u % 4:u % 4 + 1]))
                    dve.tensor_scalar(cx[:, i % 2, h, :], pv[:, i % 2, h, :], rden[:, u % 2:u % 2 + 1], None,
                                      ALU.mult).then_inc(cx_ready, 1)

                for u in range(N + 4):
                    if u < N:
                        maximum(u)
                    if 2 <= u <= N + 1:
                        normalise(u - 2)
                    if u >= 4 and u % HX == 3 and u // HX >= 1:
                        i = u // HX - 1
                        dve.wait_ge(cturned, i + 1)
                        dve.tensor_copy(cT[:].rearrange("p k c -> p (k c)"), misc[:, 0:D]).then_inc(cT_ready, 1)
                        dve.wait_ge(y_full, i + 1)
                        dve.tensor_tensor(G.branch[:, i, :], misc[:, D:2 * D], bo[:], ALU.add).then_inc(y_done, 1)


def l0_cross(nc, G):
    with ExitStack() as ctx:
        G.ctxnT = ctx.enter_context(nc.sbuf_tensor("ctxnT", [PC, 2, B * C], F32))
        context_stage(nc, G)
        l0_cross_body(nc, G)


def l0_cross_body(nc, G):
    norm_stage(nc, G, "nl", add=False, dst=G.branch,
               gain=(G.dram["L0_xattn_ln_l_g"], G.dram["L0_xattn_ln_l_b"]))
    l0_cross_attention(nc, G)


NS = 64
LO, HI = 32, 16
MAGIC = 1.5 * 2 ** 23
TWO_PI = 6.283185
CHUNKS = 8
CW = D // CHUNKS


class ConvolutionKernel:

    def __init__(self, nc, G, ctx):
        sb, ps, sem = buffers(nc, ctx, "sk")
        self.nc, self.G = nc, G
        self.par = {n: sb(n, [P, D]) for n in ("A_re", "A_im", "C_re", "C_im")}
        self.dt = sb("dt", [P, D])
        self.phase = sb("phase", [P, 1])
        self.half = sb("half", [P, 4])
        self.low, self.high = sb("low", [P, LO]), sb("high", [P, HI])
        self.ar, self.th, self.tau = sb("ar", [P, D]), sb("th", [P, D]), sb("tau", [P, D])
        self.t = [sb(f"t{i}", [P, D]) for i in range(8)]
        self.alpha, self.beta = sb("alpha", [P, D]), sb("beta", [P, D])
        self.angle = sb("angle", [P, CW, LO + 2 * HI])
        self.whole = sb("whole", [P, CW, LO + 2 * HI])
        self.grow = sb("grow", [P, CW, LO + HI])
        self.V, self.U = sb("V", [P, D, LO]), sb("U", [P, D, HI])
        self.loaded, self.dve_steps = sem("loaded"), sem("dve_steps")
        self.exp_in, self.exp_out = sem("exp_in"), sem("exp_out")
        self.sin_in, self.sin_out = sem("sin_in"), sem("sin_out")
        self.steps = [0]

    def load(self, sp):
        d = self.G.dram
        for n, to in self.par.items():
            for h in range(2):
                sp.dma_start(to[NS * h:NS * h + NS, :], d[f"L1_xattn_{n}T"]).then_inc(self.loaded, 16)
        sp.dma_start(self.dt[:], d["L1_xattn_log_dt"].partition_broadcast(P)).then_inc(self.loaded, 16)
        sp.dma_start(self.phase[:], d["c_phase"]).then_inc(self.loaded, 16)
        sp.dma_start(self.half[:], d["c_half"]).then_inc(self.loaded, 16)
        sp.dma_start(self.low[:], d["c_low"].partition_broadcast(P)).then_inc(self.loaded, 16)
        sp.dma_start(self.high[:], d["c_high"].partition_broadcast(P)).then_inc(self.loaded, 16)

    LOADS = 16 * 13

    def step(self, dve, ins):
        self.steps[0] += 1
        ins.then_inc(self.dve_steps, 1)
        dve.wait_ge(self.dve_steps, self.steps[0])

    def fraction(self, dve, x, k):
        self.step(dve, dve.tensor_scalar(k, x, MAGIC, MAGIC, ALU.add, ALU.subtract))
        return dve.tensor_tensor(x, x, k, ALU.subtract)

    def coefficients_act(self, act):
        act.wait_ge(self.loaded, self.LOADS)
        act.activation(self.dt[:], self.dt[:], ACT.Exp).then_inc(self.exp_out, 1)
        act.wait_ge(self.exp_in, 1)
        act.activation(self.t[0][:], self.ar[:], ACT.Exp).then_inc(self.exp_out, 1)
        act.activation(self.t[1][:], self.ar[:], ACT.Tanh, scale=0.5).then_inc(self.exp_out, 1)
        act.wait_ge(self.sin_in, 1)
        for x in self.t[2:5]:
            ins = act.activation(x[:], x[:], ACT.Sin, scale=TWO_PI)
        ins.then_inc(self.sin_out, 1)

    def coefficients_dve(self, dve):
        t, par, ar, th, tau, half = self.t, self.par, self.ar, self.th, self.tau, self.half
        ea, ta, cs, sn, hs = t[0:5]
        TT_, TS = dve.tensor_tensor, dve.tensor_scalar

        def step(ins):
            self.step(dve, ins)

        dve.wait_ge(self.loaded, self.LOADS)
        dve.wait_ge(self.exp_out, 1)
        TT_(ar[:], self.dt[:], par["A_re"][:], ALU.mult).then_inc(self.exp_in, 1)
        step(TT_(th[:], self.dt[:], par["A_im"][:], ALU.mult))
        step(TS(tau[:], th[:], float(1 / (2 * np.pi)), None, ALU.mult))
        step(TS(cs[:], tau[:], 0.25, None, ALU.add))
        step(TS(sn[:], tau[:], 1.0, None, ALU.mult))
        step(TS(hs[:], tau[:], 0.5, None, ALU.mult))
        for x in (cs, sn):
            step(self.fraction(dve, x[:], t[5][:]))
        self.fraction(dve, hs[:], t[5][:]).then_inc(self.sin_in, 1)
        dve.wait_ge(self.sin_in, 1)
        dve.wait_ge(self.exp_out, 3)
        step(TS(t[5][:], ea[:], 1.0, None, ALU.add))
        step(TT_(t[5][:], t[5][:], ta[:], ALU.mult))
        dve.wait_ge(self.sin_out, 1)
        step(TT_(t[5][:], t[5][:], cs[:], ALU.mult))
        step(TT_(hs[:], hs[:], hs[:], ALU.mult))
        step(dve.scalar_tensor_tensor(t[5][:], hs[:], -2.0, t[5][:], ALU.mult, ALU.add))
        step(TT_(t[6][:], ea[:], sn[:], ALU.mult))
        er, ei, A, Bm, Cr, Ci = t[5], t[6], par["A_re"], par["A_im"], par["C_re"], par["C_im"]
        step(TT_(t[0][:], A[:], A[:], ALU.mult))
        step(TT_(t[1][:], Bm[:], Bm[:], ALU.mult))
        step(TT_(t[0][:], t[0][:], t[1][:], ALU.add))
        step(dve.reciprocal(t[0][:], t[0][:]))
        step(TT_(t[1][:], er[:], A[:], ALU.mult))
        step(TT_(t[2][:], ei[:], Bm[:], ALU.mult))
        step(TT_(t[1][:], t[1][:], t[2][:], ALU.add))
        step(TT_(t[2][:], ei[:], A[:], ALU.mult))
        step(TT_(t[3][:], er[:], Bm[:], ALU.mult))
        step(TT_(t[2][:], t[2][:], t[3][:], ALU.subtract))
        step(TT_(t[1][:], t[1][:], t[0][:], ALU.mult))
        step(TT_(t[2][:], t[2][:], t[0][:], ALU.mult))
        step(TT_(t[3][:], Cr[:], t[1][:], ALU.mult))
        step(TT_(t[4][:], Ci[:], t[2][:], ALU.mult))
        step(TT_(t[3][:], t[3][:], t[4][:], ALU.subtract))
        step(TT_(t[4][:], Cr[:], t[2][:], ALU.mult))
        step(TT_(t[7][:], Ci[:], t[1][:], ALU.mult))
        step(TT_(t[4][:], t[4][:], t[7][:], ALU.add))
        step(TS(t[1][:], t[3][:], half[:, 0:1], None, ALU.mult))
        step(dve.scalar_tensor_tensor(self.alpha[:], t[4][:], half[:, 1:2], t[1][:], ALU.mult, ALU.add))
        step(TS(t[1][:], t[3][:], half[:, 2:3], None, ALU.mult))
        step(dve.scalar_tensor_tensor(self.beta[:], t[4][:], half[:, 3:4], t[1][:], ALU.mult, ALU.add))

    def column(self, x, n, c):
        return x[:, c * CW:(c + 1) * CW].unsqueeze(2).to_broadcast([P, CW, n])

    def row(self, x, n):
        return x[:].unsqueeze(1).to_broadcast([P, CW, n])

    LOW, COS, SIN = slice(0, LO), slice(LO, LO + HI), slice(LO + HI, LO + 2 * HI)

    def angles(self, dve, c):
        grow, angle = self.grow, self.angle
        dve.tensor_tensor(grow[:, :, 0:LO], self.column(self.ar, LO, c), self.row(self.low, LO), ALU.mult)
        dve.tensor_tensor(grow[:, :, LO:LO + HI], self.column(self.ar, HI, c), self.row(self.high, HI), ALU.mult
                          ).then_inc(self.exp_in, 1)
        dve.tensor_tensor(angle[:, :, self.LOW], self.column(self.tau, LO, c), self.row(self.low, LO), ALU.mult)
        self.step(dve, dve.tensor_tensor(angle[:, :, self.COS], self.column(self.tau, HI, c),
                                         self.row(self.high, HI), ALU.mult))
        dve.tensor_copy(angle[:, :, self.SIN], angle[:, :, self.COS])
        self.step(dve, dve.tensor_scalar(angle[:, :, self.LOW], angle[:, :, self.LOW], self.phase[:, 0:1], None,
                                         ALU.add))
        self.step(dve, dve.tensor_scalar(angle[:, :, self.COS], angle[:, :, self.COS], 0.25, None, ALU.add))
        self.fraction(dve, angle[:], self.whole[:]).then_inc(self.sin_in, 1)

    def functions(self, act, c):
        act.wait_ge(self.exp_in, c + 2)
        act.activation(self.grow[:], self.grow[:], ACT.Exp).then_inc(self.exp_out, 1)
        act.wait_ge(self.sin_in, c + 2)
        act.activation(self.angle[:], self.angle[:], ACT.Sin, scale=TWO_PI).then_inc(self.sin_out, 1)

    def tables(self, dve, c):
        angle, grow, mult = self.angle, self.grow, ALU.mult
        dve.wait_ge(self.exp_out, c + 4)
        dve.wait_ge(self.sin_out, c + 2)
        ch = slice(c * CW, (c + 1) * CW)
        dve.tensor_tensor(self.V[:, ch, :], angle[:, :, self.LOW], grow[:, :, 0:LO], mult)
        dve.tensor_tensor(angle[:, :, self.COS], angle[:, :, self.COS], grow[:, :, LO:], mult)
        self.step(dve, dve.tensor_tensor(angle[:, :, self.SIN], angle[:, :, self.SIN], grow[:, :, LO:], mult))
        dve.tensor_tensor(angle[:, :, self.COS], angle[:, :, self.COS], self.column(self.alpha, HI, c), mult)
        self.step(dve, dve.tensor_tensor(angle[:, :, self.SIN], angle[:, :, self.SIN],
                                         self.column(self.beta, HI, c), mult))
        self.step(dve, dve.tensor_tensor(self.U[:, ch, :], angle[:, :, self.COS], angle[:, :, self.SIN], ALU.add))

    def positions(self, nc):
        with ExitStack() as ctx:
            sb, ps, sem = buffers(nc, ctx, "sp")
            kl = sb("kl", [P, NT, D])
            pk = [ps(f"pk{i}", [LO, 32, HI]) for i in range(2)]
            summed, copied, stored = sem("summed"), sem("copied"), sem("stored")
            N = D // 32
            with nc.Block() as block:
                @block.tensor
                def _(pe):
                    for n in range(N):
                        if n >= 2:
                            pe.wait_ge(copied, n - 1)
                        for i in range(32):
                            ins = pe.matmul(pk[n % 2][:, i, :], self.V[:, 32 * n + i, :], self.U[:, 32 * n + i, :],
                                            start=True, stop=True)
                        ins.then_inc(summed, 1)

                @block.vector
                def _(dve):
                    for n in range(N):
                        dve.wait_ge(summed, n + 1)
                        for a in range(4):
                            ins = dve.tensor_copy(kl[32 * a:32 * a + 32, :, 32 * n:32 * n + 32],
                                                  pk[n % 2][:, :, :].rearrange("l c (j a) -> l a j c", a=4)[:, a])
                        ins.then_inc(copied, 1)

                @block.sync
                def _(sp):
                    sp.wait_ge(copied, N)
                    sp.dma_start(self.G.s4d_positions, kl[:].rearrange("p j d -> p (j d)")).then_inc(stored, 16)
                    sp.wait_ge(stored, 16)


E0, F0 = 8, 1024
TOP0 = 2


def l0_route(nc, G, gate):
    with ExitStack() as ctx:
        sb, ps, sem = buffers(nc, ctx, "r0")
        wr = sb("wr", [P, KD, E0])
        below = sb("below", [P, E0, E0])
        lg = sb("lg", [P, TT, E0])
        e = sb("e", [P, TT, E0])
        top = sb("top", [P, TT])
        cmp = sb("cmp", [P, TT, E0, E0])
        eq = sb("eq", [P, TT, E0, E0])
        rank = sb("rank", [P, TT, E0])
        pl = ps("pl", [P, TT, E0])
        loaded, full, shifted, exped, dve_steps = sem("loaded"), sem("full"), sem("shifted"), sem("exped"), sem("dve_steps")
        d = G.dram
        with nc.Block() as block:
            @block.sync
            def _(sp):
                sp.dma_start(wr[:], d["L0_ffn_Wr"].rearrange("(k p) n -> p k n", p=P)).then_inc(loaded, 16)
                sp.dma_start(below[:], d["c_below"].partition_broadcast(P)).then_inc(loaded, 16)

            @block.tensor
            def _(pe):
                pe.wait_ge(loaded, 32)
                for t in range(TT):
                    for k in range(KD):
                        ins = pe.matmul(pl[:, t, :], G.xT[:, k, t * P:(t + 1) * P], wr[:, k, :],
                                        start=(k == 0), stop=(k == KD - 1))
                ins.then_inc(full, 1)

            @block.scalar
            def _(act):
                act.wait_ge(shifted, 1)
                act.activation(e[:], lg[:], ACT.Exp).then_inc(exped, 1)

            @block.vector
            def _(dve):
                step = chain(dve, dve_steps)
                four = [P, TT, E0, E0]
                dve.wait_ge(loaded, 32)
                dve.wait_ge(full, 1)
                step(dve.reduce_max(top[:], pl[:], AX.X))
                dve.tensor_tensor(lg[:], pl[:], top[:].unsqueeze(2).to_broadcast([P, TT, E0]), ALU.subtract
                                  ).then_inc(shifted, 1)
                dve.wait_ge(shifted, 1)
                mine, other = lg[:].unsqueeze(3).to_broadcast(four), lg[:].unsqueeze(2).to_broadcast(four)
                dve.tensor_tensor(cmp[:], other, mine, ALU.is_gt)
                step(dve.tensor_tensor(eq[:], other, mine, ALU.is_equal))
                step(dve.tensor_tensor(eq[:], eq[:], below[:].unsqueeze(1).to_broadcast(four), ALU.mult))
                step(dve.tensor_tensor(cmp[:], cmp[:], eq[:], ALU.add))
                step(dve.reduce_sum(rank[:], cmp[:], AX.X))
                step(dve.tensor_scalar(rank[:], rank[:], float(TOP0), None, ALU.is_lt))
                dve.wait_ge(exped, 1)
                step(dve.tensor_tensor(e[:], e[:], rank[:], ALU.mult))
                step(dve.reduce_sum(top[:], e[:], AX.X))
                step(dve.reciprocal(top[:], top[:]))
                dve.tensor_tensor(gate[:], e[:].rearrange("p t e -> p e t"),
                                  top[:].unsqueeze(1).to_broadcast([P, E0, TT]), ALU.mult)


def l0_ffn(nc, G):
    with ExitStack() as outer:
        gate = buffers(nc, outer, "f0o")[0]("gate", [P, E0, TT])
        l0_route(nc, G, gate)
        kernel_of_l1 = ConvolutionKernel(nc, G, outer)
        l0_experts(nc, G, gate, kernel_of_l1)
        kernel_of_l1.positions(nc)


def l0_experts(nc, G, gate, kernel_of_l1):
    with ExitStack() as ctx:
        sb, ps, sem = buffers(nc, ctx, "f0")
        FT = F0 // P
        w1 = sb("w1", [P, 2, KD, F0])
        w2 = sb("w2", [P, 2, FT, D])
        hT = sb("hT", [P, 2, FT, S])
        ph = [ps(f"ph{i}", [P, S]) for i in range(4)]
        py = [ps(f"py{i}", [P, 512]) for i in range(4)]
        ready = sem("ready")
        first = sem("first")
        UNITS = 2 * B

        def load(sp, e, s, signal):
            sp.dma_start(w1[:, s], G.dram["L0_ffn_W1"][bass.ds(e, 1)].rearrange("a (k p) f -> p (a k) f", p=P)
                         ).then_inc(signal, 16)
            sp.dma_start(w2[:, s], G.dram["L0_ffn_W2"][bass.ds(e, 1)].rearrange("a (k p) f -> p (a k) f", p=P)
                         ).then_inc(signal, 16)

        with nc.Block() as block:
            @block.sync
            def _(sp):
                kernel_of_l1.load(sp)
                load(sp, 0, 0, first)
                sp.wait_ge(first, 32)

            @block.scalar
            def _(act):
                kernel_of_l1.coefficients_act(act)

            @block.vector
            def _(dve):
                kernel_of_l1.coefficients_dve(dve)

            @block.gpsimd
            def _(pool):
                pool.memset(G.branch[:], 0.0).then_inc(ready, 1)

        def turn(nc, it, tag, last):
            with ExitStack() as turn_ctx:
                sem, clear = turn_semaphores(nc, turn_ctx, tag)
                second, following = sem("second"), sem("following")
                h_full, h_done, y_full, y_done = sem("h_full"), sem("h_done"), sem("y_full"), sem("y_done")
                with nc.Block() as block:
                    @block.sync
                    def _(sp):
                        load(sp, it * 2 + 1, 1, second)
                        if not last:
                            sp.wait_ge(y_full, B * NT)
                            load(sp, it * 2 + 2, 0, following)
                            sp.wait_ge(following, 32)

                    @block.tensor
                    def _(pe):
                        def hidden(u):
                            s, b = u // B, u % B
                            if u == B:
                                pe.wait_ge(second, 32)
                            for f in range(FT):
                                n = u * FT + f
                                if n >= 4:
                                    pe.wait_ge(h_done, n - 3)
                                for k in range(KD):
                                    ins = pe.matmul(ph[n % 4][:], w1[:, s, k, f * P:(f + 1) * P],
                                                    G.xT[:, k, b * S:(b + 1) * S], start=(k == 0), stop=(k == KD - 1))
                                ins.then_inc(h_full, 1)

                        def out(u):
                            s = u // B
                            pe.wait_ge(h_done, (u + 1) * FT)
                            for t in range(NT):
                                n = u * NT + t
                                if n >= 4:
                                    pe.wait_ge(y_done, n - 3)
                                for f in range(FT):
                                    ins = pe.matmul(py[n % 4][:, 0:D], hT[:, u % 2, f, t * P:(t + 1) * P], w2[:, s, f, :],
                                                    start=(f == 0), stop=(f == FT - 1))
                                ins.then_inc(y_full, 1)

                        hidden(0)
                        for u in range(UNITS):
                            if u + 1 < UNITS:
                                hidden(u + 1)
                            out(u)

                    @block.scalar
                    def _(act):
                        for u in range(UNITS):
                            if u >= 2:
                                act.wait_ge(y_full, (u - 1) * NT)
                            for f in range(FT):
                                n = u * FT + f
                                act.wait_ge(h_full, n + 1)
                                act.activation(hT[:, u % 2, f, :], ph[n % 4][:], ACT.Relu).then_inc(h_done, 1)
                            if last:
                                kernel_of_l1.functions(act, u)

                    @block.vector
                    def _(dve):
                        if last:
                            kernel_of_l1.angles(dve, 0)
                            kernel_of_l1.tables(dve, 0)
                            kernel_of_l1.angles(dve, 1)
                        for u in range(UNITS):
                            s, b = u // B, u % B
                            if last and 1 <= u:
                                kernel_of_l1.tables(dve, u)
                                if u + 1 < CHUNKS:
                                    kernel_of_l1.angles(dve, u + 1)
                            for t in range(NT):
                                n, tile = u * NT + t, b * NT + t
                                dve.wait_ge(y_full, n + 1)
                                if u == B:
                                    dve.wait_ge(y_done, n - B * NT + 1)
                                g = gate[:, bass.ds(it * 2 + s, 1), tile:tile + 1].rearrange("p a b -> p (a b)")
                                dve.scalar_tensor_tensor(G.branch[:, tile, :], py[n % 4][:, 0:D], g,
                                                         G.branch[:, tile, :], ALU.mult, ALU.add).then_inc(y_done, 1)
                clear()

        with nc.Fori(0, E0 // 2 - 1) as it:
            turn(nc, it, "f0t", False)
        turn(nc, E0 // 2 - 1, "f0l", True)


H1, DH1 = 16, 64
INNER1 = H1 * DH1
MEM = 16
TOP1 = 64
R8 = P // H1
NR = P // R8
HIDE = -1e30
GONE = -3e38


def l1_attention(nc, G):
    with ExitStack() as ctx:
        sb, ps, sem = buffers(nc, ctx, "a1")
        KK = INNER1 // P
        wo = sb("wo", [P, KK, D])
        ones = sb("ones", [1, P])
        eye8 = sb("eye8", [P, R8])
        cut8 = sb("cut8", [P, R8])
        mixes = sb("mixes", [P, 2, H1])
        kpre = sb("kpre", [P, H1, R8])
        kpost = sb("kpost", [P, H1, R8])
        kp = sb("kp", [P, 2, P])
        mkT = sb("mkT", [P, KK, MEM])
        side = sb("side", [64, INNER1])
        bo, mv = side[0:1, 0:D], side[32:32 + MEM, :]
        qT = sb("qT", [P, KK, S])
        kT = sb("kT", [P, KK, S])
        v = sb("v", [P, NT, INNER1])
        dT = sb("dT", [P, NT, NR, P])
        aT = sb("aT", [P, NT, H1, P])
        edge = sb("edge", [64, H1 * P])
        dM = edge[0:MEM].rearrange("p (r c) -> p r c", r=NR)
        aM = edge[32:32 + MEM].rearrange("p (h c) -> p h c", h=H1)
        rows = sb("rows", [P, 2, MEM + S])
        mixed = sb("mixed", [P, 4, MEM + S])
        rest = sb("rest", [P, 2, MEM + S])
        probs = sb("probs", [P, 2, MEM + S])
        best = sb("best", [P, 2, TOP1 // 8, 8])
        negmax = sb("negmax", [P, 2])
        den = sb("den", [P, 2])
        rden = sb("rden", [P, 2])
        cT = aT[:, NT - 1, 0:KK, :]
        spare = dT[:].rearrange("p a h c -> p (a h c)")
        W1 = KD * INNER1
        wqkv = [spare[:, n * W1:(n + 1) * W1].rearrange("p (k n) -> p k n", k=KD) for n in range(3)]
        xb = spare[:, 3 * W1:3 * W1 + KD * S].rearrange("p (k n) -> p k n", k=KD)

        pd = [ps(f"pd{i}", [P, 512]) for i in range(2)]
        ptr = ps("ptr", [P, 1024])
        pmix = ps("pmix", [P, 1024])
        pat = ps("pat", [P, 8, P])
        loaded, kron, early = sem("loaded"), sem("kron"), sem("early")
        filled, emptied = sem("filled"), sem("emptied")
        d = G.dram

        scale = DH1 ** -0.5

        NG = NT * NR
        tokens = [(g // NR) * P + R8 * (g % NR + 1) for g in range(NG)]
        width = [MEM + n for n in tokens]
        searched = [n > TOP1 for n in width]
        PAIRS = NG // 2
        BANK = 512
        SPLIT = MEM + 3 * P + 96

        def pieces(n):
            return [(0, n, 0)] if n <= BANK else [(0, SPLIT, 0), (SPLIT, n, BANK)]

        def place(col, n):
            return col if n <= BANK or col < SPLIT else BANK + col - SPLIT

        def load_weights(sp, signals):
            for n, name in enumerate(("Wq", "Wk", "Wv")):
                sp.dma_start(wqkv[n], d[f"L1_attn_{name}"].rearrange("(k p) n -> p k n", p=P)).then_inc(signals[n], 16)

        def project(pe, which, m, out, b):
            for k in range(KD):
                ins = pe.matmul(out[:], wqkv[which][:, k, m * P:(m + 1) * P], G.xT[:, k, bass.ds(b * S, S)],
                                start=(k == 0), stop=(k == KD - 1))
            return ins

        LOADS = 16 * (4 + 2 * H1 + 3)
        with nc.Block() as block:
            @block.sync
            def _(sp):
                load_weights(sp, [early, early, early])
                sp.dma_start(wo[:], d["L1_attn_Wo"].rearrange("(k p) n -> p k n", p=P)).then_inc(loaded, 16)
                sp.dma_start(bo, d["L1_attn_bo"].rearrange("(a n) -> a n", a=1)).then_inc(loaded, 16)
                sp.dma_start(eye8[:], d["c_eye8"]).then_inc(loaded, 16)
                sp.dma_start(cut8[:], d["c_cut8"]).then_inc(loaded, 16)
                for n, name in enumerate(("pre", "post")):
                    for h in range(H1):
                        sp.dma_start(mixes[R8 * h:R8 * h + R8, n, :],
                                     d[f"L1_attn_{name}_proj"][h].partition_broadcast(R8)).then_inc(loaded, 16)
                for half in range(2):
                    sp.dma_start(mkT[64 * half:64 * half + 64, :, :],
                                 d["L1_attn_mem_kT"].rearrange("(c a) d m -> a d c m", a=2)[half]).then_inc(loaded, 16)
                sp.dma_start(mv.rearrange("m (h d) -> m h d", h=H1),
                             d["L1_attn_mem_v"].rearrange("h m d -> m h d")).then_inc(loaded, 16)

            @block.vector
            def _(dve):
                dve.memset(ones[:], 1.0).then_inc(kron, 1)
                dve.wait_ge(loaded, LOADS)
                for n, to in enumerate((kpre, kpost)):
                    dve.tensor_tensor(to[:], mixes[:, n, :].unsqueeze(2).to_broadcast([P, H1, R8]),
                                      eye8[:].unsqueeze(1).to_broadcast([P, H1, R8]), ALU.mult).then_inc(kron, 1)

            @block.tensor
            def _(pe):
                pe.wait_ge(early, 48)
                for n in range(2 * KK):
                    if n >= 2:
                        pe.wait_ge(emptied, n - 1)
                    project(pe, n // KK, n % KK, pd[n % 2], 0).then_inc(filled, 1)

            @block.scalar
            def _(act):
                for n in range(2 * KK):
                    act.wait_ge(filled, n + 1)
                    act.copy((qT, kT)[n // KK][:, n % KK, :], pd[n % 2][:]).then_inc(emptied, 1)

            @block.gpsimd
            def _(pool):
                pool.tensor_copy(xb, G.xT[:, :, 0:S])

        def turn_of_batch(nc, b, tag, last):
            turn_ctx = ExitStack()
            sem, clear = turn_semaphores(nc, turn_ctx, tag)
            w_loaded = [sem(f"w{x}_loaded") for x in "qkv"]
            pd_full, pd_free, tr_full, rows_ready = sem("pd_full"), sem("pd_free"), sem("tr_full"), sem("rows_ready")
            mix_full, mixed_ready, max_ready, exp_ready = sem("mix_full"), sem("mixed_ready"), sem("max_ready"), sem("exp_ready")
            sums_ready, kp_ready, post_full, aT_ready = sem("sums_ready"), sem("kp_ready"), sem("post_full"), sem("aT_ready")
            zeroed, dve_steps = sem("zeroed"), sem("dve_steps")
            with nc.Block() as block:
                @block.sync
                def _(sp):
                    if not last:
                        sp.wait_ge(tr_full, NG)
                        load_weights(sp, w_loaded)
                        sp.wait_ge(w_loaded[2], 16)

                @block.tensor
                def _(pe):
                    n = [0]

                    def bank():
                        pe.wait_ge(pd_free, max(n[0] - 1, 0))
                        return pd[n[0] % 2]

                    def full(ins):
                        ins.then_inc(pd_full, 1)
                        n[0] += 1

                    def project_next(which):
                        pe.wait_ge(w_loaded[which], 16)
                        for m in range(KK):
                            full(project(pe, which, m, bank(), b + 1))

                    def values():
                        for j in range(NT):
                            for m in range(INNER1 // 512):
                                out = bank()
                                for k in range(KD):
                                    ins = pe.matmul(out[:], xb[:, k, j * P:(j + 1) * P],
                                                    wqkv[2][:, k, m * 512:(m + 1) * 512],
                                                    start=(k == 0), stop=(k == KD - 1))
                                full(ins)

                    def scores(i):
                        for ch in list(range(i + 1)) + [NT]:
                            for quad in range(4):
                                out = bank()
                                for a in range(4):
                                    h = 8 * (quad // 2) + 2 * a + quad % 2
                                    r, kk = slice(64 * (h % 2), 64 * (h % 2) + 64), h // 2
                                    keys = kT[r, kk, ch * P:(ch + 1) * P] if ch < NT else mkT[r, kk, :]
                                    m = P if ch < NT else MEM
                                    ins = pe.matmul(out[0:m, a * P:(a + 1) * P], keys, qT[r, kk, i * P:(i + 1) * P],
                                                    start=True, stop=True)
                                full(ins)
                        fills_of_scores[i] = n[0]

                    def turn(g):
                        i, r = g // NR, g % NR
                        pe.wait_ge(pd_free, fills_of_scores[i])
                        pe.wait_ge(rows_ready, g)
                        pe.transpose(ptr[:, 0:MEM], dM[:, r, :], G.ident[0:MEM, 0:MEM])
                        for ch in range(i + 1):
                            col = MEM + ch * P
                            nk = min(P, tokens[g] - ch * P)
                            cuts = [(0, nk)] if width[g] <= BANK or ch < 3 else [(0, 96), (96, nk)]
                            for lo, hi in cuts:
                                at = place(col + lo, width[g])
                                ins = pe.transpose(ptr[:, at:at + hi - lo], dT[lo:hi, ch, r, :],
                                                   G.ident[lo:hi, lo:hi])
                        ins.then_inc(tr_full, 1)

                    def mix(g):
                        pe.wait_ge(rows_ready, g + 1)
                        pe.wait_ge(mixed_ready, g)
                        w = width[g]
                        for lo, hi, at in pieces(w):
                            pe.matmul(pmix[:, at:at + hi - lo], kpre[:].rearrange("p h q -> p (h q)"),
                                      rows[:, g % 2, lo:hi], start=True, stop=(hi != w))
                        at = place(w - R8, w)
                        pe.matmul(pmix[:, at:at + R8], G.ident[:], cut8[:], start=False, stop=True).then_inc(mix_full, 1)

                    def post(g):
                        i = g // NR
                        pe.wait_ge(kp_ready, g + 1)
                        pe.wait_ge(aT_ready, g)
                        for ch in range(i + 1):
                            pe.matmul(pat[:, ch, :], probs[:, g % 2, MEM + ch * P:MEM + (ch + 1) * P], kp[:, g % 2, :],
                                      start=True, stop=True)
                        pe.matmul(pat[32:32 + MEM, NT, :], probs[:, g % 2, 0:MEM], kp[:, g % 2, :],
                                  start=True, stop=True).then_inc(post_full, 1)

                    def output(i):
                        pe.wait_ge(aT_ready, NR * (i + 1))
                        for half in range(2):
                            out = bank()
                            for a in range(8):
                                h = 8 * half + a
                                to = out[64 * (h % 2):64 * (h % 2) + 64, (a // 2) * P:(a // 2 + 1) * P]
                                hc = slice(h * DH1, (h + 1) * DH1)
                                for ch in range(i + 1):
                                    pe.matmul(to, v[:, ch, hc], aT[:, ch, h, :], start=(ch == 0), stop=False)
                                ins = pe.matmul(to, mv[:, hc], aM[:, h, :], start=False, stop=True)
                            full(ins)
                        pe.wait_ge(pd_free, n[0])
                        out = bank()
                        for kk in range(KK):
                            pe.matmul(out[:, 0:D], cT[:, kk, :], wo[:, kk, :], start=(kk == 0), stop=False)
                        full(pe.matmul(out[:, 0:D], ones[:], bo, start=False, stop=True))

                    fills_of_scores = [0] * NT
                    for k in range(-2, PAIRS + 1):
                        for a in range(2):
                            if k >= 1:
                                post(2 * (k - 1) + a)
                            if 0 <= k + 1 < PAIRS:
                                mix(2 * (k + 1) + a)
                        if k >= 1 and (k - 1) % (NR // 2) == NR // 2 - 1:
                            output((k - 1) // (NR // 2))
                        if k + 2 < PAIRS:
                            if (k + 2) % (NR // 2) == 0:
                                scores((k + 2) // (NR // 2))
                            for a in range(2):
                                turn(2 * (k + 2) + a)
                        elif k < PAIRS and not last:
                            project_next(k + 2 - PAIRS)
                        if k == 5:
                            values()

                @block.scalar
                def _(act):
                    n = [0]

                    def empty(to, src):
                        act.wait_ge(pd_full, n[0] + 1)
                        act.copy(to, src(pd[n[0] % 2])).then_inc(pd_free, 1)
                        n[0] += 1

                    def scores(i):
                        act.wait_ge(tr_full, i * NR)
                        for ch in list(range(i + 1)) + [NT]:
                            m = P if ch < NT else MEM
                            for quad in range(4):
                                to = dT[:, ch] if ch < NT else dM
                                to = to[:].rearrange("p r (z a y q) -> p z y a r q", z=2, a=4, y=2)[:, quad // 2, quad % 2]
                                empty(to, lambda bank, m=m: bank[0:m, :].rearrange("p (a r q) -> p a r q", a=4, r=NR))

                    def turned(g):
                        act.wait_ge(tr_full, g + 1)
                        act.wait_ge(mix_full, max(g - 1, 0))
                        for lo, hi, at in pieces(width[g]):
                            ins = act.copy(rows[:, g % 2, lo:hi], ptr[:, at:at + hi - lo])
                        ins.then_inc(rows_ready, 1)

                    def mixed_out(g):
                        act.wait_ge(mix_full, g + 1)
                        act.wait_ge(sums_ready, max(g - 3, 0))
                        for lo, hi, at in pieces(width[g]):
                            ins = act.copy(mixed[:, g % 4, lo:hi], pmix[:, at:at + hi - lo])
                        ins.then_inc(mixed_ready, 1)

                    def exps(g):
                        act.wait_ge(max_ready, g + 1)
                        act.wait_ge(post_full, max(g - 1, 0))
                        act.wait_ge(zeroed, 2 * (g // NR) + min(g % NR + 1, 2))
                        act.activation(probs[:, g % 2, 0:width[g]], mixed[:, g % 4, 0:width[g]], ACT.Exp,
                                       bias=negmax[:, g % 2:g % 2 + 1], scale=scale).then_inc(exp_ready, 1)

                    def post_out(g):
                        i, r = g // NR, g % NR
                        q = slice(R8 * r, R8 * r + R8)
                        act.wait_ge(post_full, g + 1)
                        act.copy(aT[:, 0:i + 1, :, q], pat[:, 0:i + 1, :].rearrange("p c (h q) -> p c h q", h=H1))
                        act.copy(aM[:, :, q], pat[32:32 + MEM, NT, :].rearrange("p (h q) -> p h q", h=H1)
                                 ).then_inc(aT_ready, 1)

                    def output(i):
                        for half in range(2):
                            empty(cT[:, 4 * half:4 * half + 4, :].rearrange("p k c -> p (k c)"), lambda bank: bank[:])
                        empty(G.branch[:, bass.ds(b * NT + i, 1), :].rearrange("p a d -> p (a d)"),
                              lambda bank: bank[:, 0:D])

                    for k in range(-2, PAIRS + 1):
                        for a in range(2):
                            if k >= 1:
                                post_out(2 * (k - 1) + a)
                            if 0 <= k < PAIRS:
                                exps(2 * k + a)
                            if 0 <= k + 1 < PAIRS:
                                mixed_out(2 * (k + 1) + a)
                        if k >= 1 and (k - 1) % (NR // 2) == NR // 2 - 1:
                            output((k - 1) // (NR // 2))
                        if k + 2 < PAIRS:
                            if (k + 2) % (NR // 2) == 0:
                                scores((k + 2) // (NR // 2))
                            for a in range(2):
                                turned(2 * (k + 2) + a)
                        elif k < PAIRS and not last:
                            for m in range(KK):
                                empty((qT, kT)[k + 2 - PAIRS][:, m, :], lambda bank: bank[:])
                        if k == 5:
                            for j in range(NT):
                                for m in range(INNER1 // 512):
                                    empty(v[:, j, m * 512:(m + 1) * 512], lambda bank: bank[:])

                @block.gpsimd
                def _(pool):
                    for g in range(NG):
                        i = g // NR
                        if g % NR == 0:
                            for a in range(2):
                                pool.wait_ge(post_full, max(g + a - 1, 0))
                                pool.memset(probs[:, a, MEM + i * P:MEM + (i + 1) * P], 0.0).then_inc(zeroed, 1)
                        pool.wait_ge(sums_ready, g + 1)
                        pool.wait_ge(post_full, max(g - 1, 0))
                        pool.tensor_scalar(kp[:, g % 2, :], kpost[:].rearrange("p h q -> p (h q)"),
                                           rden[:, g % 2:g % 2 + 1], None, ALU.mult).then_inc(kp_ready, 1)
                    if not last:
                        pool.wait_ge(tr_full, NG)
                        pool.tensor_copy(xb, G.xT[:, :, bass.ds((b + 1) * S, S)])

                @block.vector
                def _(dve):
                    count = [0]

                    def signal(ins):
                        count[0] += 1
                        ins.then_inc(dve_steps, 1)
                        return count[0]

                    def after(step):
                        dve.wait_ge(dve_steps, step)

                    for pair in range(PAIRS):
                        lanes = [(a, 2 * pair + a, width[2 * pair + a]) for a in range(2)]
                        last = [0, 0]
                        rows_of = [mixed[:, g % 4, 0:w] for _, g, w in lanes]
                        floor = [GONE, GONE]
                        for a, g, w in lanes:
                            dve.wait_ge(mixed_ready, g + 1)
                            last[a] = signal(dve.max(best[:, a, 0, :], rows_of[a]))
                        for a, g, w in lanes:
                            after(last[a])
                            dve.tensor_scalar(negmax[:, a:a + 1], best[:, a, 0, 0:1], -scale, None, ALU.mult
                                              ).then_inc(max_ready, 1)
                        if searched[2 * pair]:
                            for q in range(1, TOP1 // 8):
                                for a, g, w in lanes:
                                    after(last[a])
                                    last[a] = signal(dve.match_replace(
                                        rest[:, a, 0:w], best[:, a, q - 1, :], rows_of[a] if q == 1 else rest[:, a, 0:w],
                                        GONE))
                                for a, g, w in lanes:
                                    after(last[a])
                                    last[a] = signal(dve.max(best[:, a, q, :], rest[:, a, 0:w]))
                            floor = [best[:, a, TOP1 // 8 - 1, 7:8] for a in range(2)]
                        for a, g, w in lanes:
                            dve.wait_ge(exp_ready, g + 1)
                            dve.wait_ge(kp_ready, max(g - 1, 0))
                            after(last[a])
                            last[a] = signal(dve.scalar_tensor_tensor(probs[:, a, 0:w], rows_of[a], floor[a],
                                                                      probs[:, a, 0:w], ALU.is_ge, ALU.mult,
                                                                      accum_out=den[:, a:a + 1]))
                        for a, g, w in lanes:
                            after(last[a])
                            dve.reciprocal(rden[:, a:a + 1], den[:, a:a + 1]).then_inc(sums_ready, 1)
            turn_ctx.close()
            clear()

        with nc.Fori(0, B - 1) as b:
            turn_of_batch(nc, b, "a1t", False)
        turn_of_batch(nc, B - 1, "a1l", True)


HV, DV = 4, 32
TOPV = 32
FR = 512
FT = FR // P


def s4d_spectrum(nc, G, kf):
    with ExitStack() as ctx:
        sb, ps, sem = buffers(nc, ctx, "ss")
        kl = sb("kl", [P, NT, D])
        dft = sb("dft", [P, NT, 2 * FR])
        pf = [ps(f"pf{i}", [P, 512]) for i in range(2)]
        loaded, spectrum, stored = sem("loaded"), sem("spectrum"), sem("stored")
        with nc.Block() as block:
            @block.sync
            def _(sp):
                sp.dma_start(kl[:], G.s4d_positions.rearrange("p (j d) -> p j d", j=NT)).then_inc(loaded, 16)
                sp.dma_start(dft[:], G.dram["c_dft"].rearrange("(k p) f -> p k f", p=P)).then_inc(loaded, 16)

            @block.scalar
            def _(act):
                for n in range(2 * FT):
                    act.wait_ge(spectrum, n + 1)
                    act.copy(kf[:, n, :], pf[n % 2][:, 0:D]).then_inc(stored, 1)

            @block.tensor
            def _(pe):
                pe.wait_ge(loaded, 32)
                for m in range(2 * FT):
                    if m >= 2:
                        pe.wait_ge(stored, m - 1)
                    for k in range(NT):
                        ins = pe.matmul(pf[m % 2][:, 0:D], dft[:, k, m * P:(m + 1) * P], kl[:, k, :],
                                        start=(k == 0), stop=(k == NT - 1))
                    ins.then_inc(spectrum, 1)


def modulation_attention(nc, G, cT):
    with ExitStack() as ctx:
        sb, ps, sem = buffers(nc, ctx, "ma")
        wq = sb("wq", [P, KD, HV * DV])
        wk = sb("wk", [PC, 2, HV * DV])
        wv = sb("wv", [PC, 2, D])
        vmask = sb("vmask", [1, B * C], U8)
        tmask = sb("tmask", [P, TT], U8)
        keep = sb("keep", [P, TT])
        hide = sb("hide", [1, B, HV, C])
        ones = sb("ones", [1, P])
        qT = sb("qT", [P, B * S])
        kd = sb("kd", [P, B, HV, C])
        v = sb("v", [C, B, D])
        sc = sb("sc", [P, 2, HV, C])
        rest = sb("rest", [P, 2, HV, C])
        best = sb("best", [P, TOPV // 8, HV, 8])
        e = sb("e", [P, 2, HV, C])
        den = sb("den", [P, HV])
        mean = sb("mean", [P, 2, C])
        mT = sb("mT", [C, B * S])
        pp = [ps(f"pp{i}", [P, 512]) for i in range(2)]
        psc = [ps(f"psc{i}", [P, 512]) for i in range(2)]
        pt = [ps(f"pt{i}", [P, 512]) for i in range(2)]
        loaded, hidden, cleared = sem("loaded"), sem("hidden"), sem("cleared")
        full, emptied, kfull, kready = sem("full"), sem("emptied"), sem("kfull"), sem("kready")
        scored, shifted, exped, meaned, turned, stored = (
            sem("scored"), sem("shifted"), sem("exped"), sem("meaned"), sem("turned"), sem("stored"))
        dve_steps, mixed, cstored = sem("dve_steps"), sem("mixed"), sem("cstored")
        d = G.dram
        scale = DV ** -0.5
        with nc.Block() as block:
            @block.sync
            def _(sp):
                sp.dma_start(wq[:], d["L1_xattn_Wq"].rearrange("(k p) n -> p k n", p=P)).then_inc(loaded, 16)
                sp.dma_start(wk[:], d["L1_xattn_Wk"].rearrange("(k p) n -> p k n", p=PC)).then_inc(loaded, 16)
                sp.dma_start(wv[:], d["L1_xattn_Wv"].rearrange("(k p) n -> p k n", p=PC)).then_inc(loaded, 16)
                sp.dma_start(vmask[:], d["mask_BxS2_bf1"].rearrange("(a b) c -> a (b c)", a=1)).then_inc(loaded, 16)
                with nc.allow_non_contiguous_dma(reason="2048 bytes of a mask onto partitions"):
                    for b in range(B):
                        sp.dma_start(tmask[:, b * NT:(b + 1) * NT],
                                     d["mask_BxS_bf1"][b].rearrange("(t p) -> p t", p=P)).then_inc(loaded, 16)

            @block.tensor
            def _(pe):
                pe.wait_ge(loaded, 128)
                for n in range(B):
                    if n >= 2:
                        pe.wait_ge(emptied, n - 1)
                    for k in range(KD):
                        ins = pe.matmul(pp[n % 2][:], wq[:, k, :], G.xT[:, k, n * S:(n + 1) * S],
                                        start=(k == 0), stop=(k == KD - 1))
                    ins.then_inc(full, 1)
                for b in range(B):
                    n = B + b
                    pe.wait_ge(emptied, n - 1)
                    for k in range(2):
                        ins = pe.matmul(pp[n % 2][0:C, 0:D], G.ctxT[:, k, b * C:(b + 1) * C], wv[:, k, :],
                                        start=(k == 0), stop=(k == 1))
                    ins.then_inc(full, 1)
                for k in range(2):
                    ins = pe.matmul(psc[1][:, 0:B * C], wk[:, k, :], G.ctxT[:, k, :], start=(k == 0), stop=(k == 1))
                ins.then_inc(kfull, 1)
                pe.wait_ge(kready, 1)
                pe.wait_ge(emptied, 2 * B)
                pe.wait_ge(hidden, 6)

                def scores(i):
                    if i >= 2:
                        pe.wait_ge(shifted, i - 1)
                    b = i // NT
                    pe.matmul(psc[i % 2][:, 0:HV * C], qT[:, i * P:(i + 1) * P],
                              kd[:, b].rearrange("p h c -> p (h c)"), start=True, stop=False)
                    pe.matmul(psc[i % 2][:, 0:HV * C], ones[:], hide[:, b].rearrange("p h c -> p (h c)"),
                              start=False, stop=True).then_inc(scored, 1)

                def turn(i):
                    pe.wait_ge(meaned, i + 1)
                    if i >= 2:
                        pe.wait_ge(stored, i - 1)
                    pe.transpose(pt[i % 2][0:C, 0:P], mean[:, i % 2, :], G.ident[:]).then_inc(turned, 1)

                scores(0)
                scores(1)
                for i in range(TT):
                    if i + 2 < TT:
                        scores(i + 2)
                    turn(i)
                for n in range(B * KD):
                    b, k = n // KD, n % KD
                    if n == 0:
                        pe.wait_ge(stored, TT)
                    if n >= 2:
                        pe.wait_ge(cstored, n - 1)
                    pe.matmul(pp[n % 2][:], v[:, b, k * P:(k + 1) * P], mT[:, b * S:(b + 1) * S],
                              start=True, stop=True).then_inc(mixed, 1)

            @block.gpsimd
            def _(pool):
                pool.memset(kd[:], 0.0).then_inc(cleared, 1)

            @block.scalar
            def _(act):
                for n in range(2 * B):
                    act.wait_ge(full, n + 1)
                    if n < B:
                        ins = act.copy(qT[:, n * S:(n + 1) * S], pp[n % 2][:])
                    else:
                        ins = act.copy(v[:, n - B, :], pp[n % 2][0:C, 0:D])
                    ins.then_inc(emptied, 1)
                act.wait_ge(kfull, 1)
                act.wait_ge(cleared, 1)
                for h in range(HV):
                    r = slice(DV * h, DV * h + DV)
                    ins = act.copy(kd[r, :, h, :], psc[1][r, 0:B * C].rearrange("p (b c) -> p b c", b=B))
                ins.then_inc(kready, 1)
                for i in range(TT + 1):
                    if i < TT:
                        act.wait_ge(shifted, i + 1)
                        if i >= 2:
                            act.wait_ge(meaned, i - 1)
                        act.activation(e[:, i % 2], sc[:, i % 2], ACT.Exp, scale=scale).then_inc(exped, 1)
                    if i >= 1:
                        j = i - 1
                        act.wait_ge(turned, j + 1)
                        act.copy(mT[:, j * P:(j + 1) * P], pt[j % 2][0:C, 0:P]).then_inc(stored, 1)
                for n in range(B * KD):
                    act.wait_ge(mixed, n + 1)
                    act.copy(cT[:, n % KD, (n // KD) * S:(n // KD + 1) * S], pp[n % 2][:]).then_inc(cstored, 1)

            @block.vector
            def _(dve):
                step = chain(dve, dve_steps)
                dve.wait_ge(loaded, 128)
                dve.memset(ones[:], 1.0).then_inc(hidden, 1)
                dve.tensor_copy(keep[:], tmask[:]).then_inc(hidden, 1)
                dve.tensor_copy(hide[:, :, 0, :].rearrange("p b c -> p b c"),
                                vmask[:].rearrange("p (b c) -> p b c", b=B)).then_inc(hidden, 1)
                dve.wait_ge(hidden, 3)
                dve.tensor_scalar(hide[:, :, 0, :], hide[:, :, 0, :], 1.0, -HIDE, ALU.subtract, ALU.mult
                                  ).then_inc(hidden, 1)
                dve.wait_ge(hidden, 4)
                dve.tensor_copy(hide[:, :, 1, :], hide[:, :, 0, :]).then_inc(hidden, 1)
                dve.wait_ge(hidden, 5)
                dve.tensor_copy(hide[:, :, 2:4, :], hide[:, :, 0:2, :]).then_inc(hidden, 1)
                four = [P, HV, C]

                def search(i):
                    dve.wait_ge(scored, i + 1)
                    if i >= 2:
                        dve.wait_ge(exped, i - 1)
                    flat = sc[:, i % 2].rearrange("p h c -> p (h c)")
                    step(dve.tensor_copy(flat, psc[i % 2][:, 0:HV * C]))
                    for q in range(TOPV // 8):
                        for h in range(HV):
                            src = sc[:, i % 2, h, :] if q == 0 else rest[:, i % 2, h, :]
                            ins = dve.max(best[:, q, h, :], src)
                        step(ins)
                        for h in range(HV):
                            src = sc[:, i % 2, h, :] if q == 0 else rest[:, i % 2, h, :]
                            ins = dve.match_replace(rest[:, i % 2, h, :], best[:, q, h, :], src, GONE)
                        step(ins)
                    dve.tensor_tensor(sc[:, i % 2], sc[:, i % 2], best[:, 0, :, 0:1].to_broadcast(four),
                                      ALU.subtract).then_inc(shifted, 1)

                def average(i):
                    dve.wait_ge(exped, i + 1)
                    if i >= 2:
                        dve.wait_ge(turned, i - 1)
                    ei, ri = (x[:, i % 2].rearrange("p h c -> p (h c)") for x in (e, rest))
                    step(dve.scalar_tensor_tensor(ei, ri, GONE, ei, ALU.is_equal, ALU.mult))
                    step(dve.reduce_sum(den[:], e[:, i % 2], AX.X))
                    step(dve.tensor_scalar(den[:], den[:], float(HV), None, ALU.mult))
                    step(dve.reciprocal(den[:], den[:]))
                    step(dve.tensor_tensor(e[:, i % 2], e[:, i % 2], den[:].unsqueeze(2).to_broadcast(four), ALU.mult))
                    step(dve.reduce_sum(mean[:, i % 2, :], e[:, i % 2].rearrange("p h c -> p c h"), AX.X))
                    dve.tensor_scalar(mean[:, i % 2, :], mean[:, i % 2, :], keep[:, i:i + 1], None, ALU.mult
                                      ).then_inc(meaned, 1)

                search(0)
                for i in range(TT):
                    if i + 1 < TT:
                        search(i + 1)
                    average(i)


def modulate(nc, G, cT):
    with ExitStack() as ctx:
        sb, ps, sem = buffers(nc, ctx, "mo")
        w = sb("w", [P, KD, 2 * D])
        bias = sb("bias", [1, 2 * D])
        ones = sb("ones", [1, P])
        g = sb("g", [P, D])
        bb = sb("bb", [P, D])
        gate = sb("gate", [P, 1])
        s1 = sb("s1", [P, 2, D])
        h1 = sb("h1", [P, 2, D])
        pw = [ps(f"pw{i}", [P, 512]) for i in range(2)]
        loaded, one, full, emptied, done, dve_steps = (
            sem("loaded"), sem("one"), sem("full"), sem("emptied"), sem("done"), sem("dve_steps"))
        scaled, gained = sem("scaled"), sem("gained")
        d = G.dram
        with nc.Block() as block:
            @block.sync
            def _(sp):
                sp.dma_start(w[:], d["L1_xattn_W_film_in"].rearrange("(k p) n -> p k n", p=P)).then_inc(loaded, 16)
                sp.dma_start(bias[:], d["L1_xattn_b_film_in"].rearrange("(a n) -> a n", a=1)).then_inc(loaded, 16)
                sp.dma_start(g[:], d["L1_xattn_g_norm_in"].partition_broadcast(P)).then_inc(loaded, 16)
                sp.dma_start(bb[:], d["L1_xattn_b_norm_in"].partition_broadcast(P)).then_inc(loaded, 16)
                sp.dma_start(gate[:], d["L1_xattn_mod_gate"].partition_broadcast(P)).then_inc(loaded, 16)

            @block.tensor
            def _(pe):
                pe.wait_ge(loaded, 80)
                pe.wait_ge(one, 1)
                for i in range(TT):
                    if i >= 2:
                        pe.wait_ge(emptied, i - 1)
                    film_product(pe, pw[i % 2], cT, w, ones, bias, i).then_inc(full, 1)

            @block.gpsimd
            def _(pool):
                pool.wait_ge(loaded, 80)
                for i in range(TT):
                    x = G.branch[:, i, :]
                    pool.tensor_tensor(x, x, g[:], ALU.mult).then_inc(scaled, 1)
                    pool.wait_ge(scaled, i + 1)
                    pool.tensor_tensor(x, x, bb[:], ALU.add).then_inc(gained, 1)

            @block.vector
            def _(dve):
                step = chain(dve, dve_steps)
                dve.memset(ones[:], 1.0).then_inc(one, 1)
                dve.wait_ge(loaded, 80)
                for i in range(TT):
                    dve.wait_ge(full, i + 1)
                    dve.tensor_scalar(s1[:, i % 2], pw[i % 2][:, 0:D], gate[:, 0:1], 1.0, ALU.mult, ALU.add)
                    ins = dve.tensor_scalar(h1[:, i % 2], pw[i % 2][:, D:2 * D], gate[:, 0:1], None, ALU.mult)
                    ins.then_inc(emptied, 1)
                    dve.wait_ge(emptied, i + 1)
                    dve.wait_ge(gained, i + 1)
                    x = G.branch[:, i, :]
                    step(dve.tensor_tensor(x, x, s1[:, i % 2], ALU.mult))
                    dve.tensor_tensor(x, x, h1[:, i % 2], ALU.add)


def film_product(pe, out, cT, w, ones, bias, i):
    for k in range(KD):
        pe.matmul(out[:], cT[:, k, i * P:(i + 1) * P], w[:, k, :], start=(k == 0), stop=False)
    return pe.matmul(out[:], ones[:], bias[:], start=False, stop=True)


def convolve(nc, G, cT, kf):
    with ExitStack() as ctx:
        sb, ps, sem = buffers(nc, ctx, "cv")
        dft = sb("dft", [P, NT, 2 * FR])
        inv = sb("inv", [P, 2 * FT, S])
        w = sb("w", [P, KD, 2 * D])
        bias = sb("bias", [1, 2 * D])
        ones = sb("ones", [1, P])
        skip = sb("skip", [P, D])
        gate = sb("gate", [P, 1])
        spec = sb("spec", [P, 2 * FT, 2 * D])
        prod = sb("prod", [P, 2, 4, 2 * D])
        y = sb("y", [P, 2, 2, D])
        sk = sb("sk", [P, 2, 2, D])
        s1 = sb("s1", [P, D])
        h1 = sb("h1", [P, D])
        pf = [ps(f"pf{i}", [P, 2, 512]) for i in range(2)]
        py = [ps(f"py{i}", [P, 512]) for i in range(2)]
        pw = [ps(f"pw{i}", [P, 512]) for i in range(2)]
        loaded, one, xfull, xread, ready = sem("loaded"), sem("one"), sem("xfull"), sem("xread"), sem("ready")
        yfull, yread, wfull, wread, dve_steps, skipped = (
            sem("yfull"), sem("yread"), sem("wfull"), sem("wread"), sem("dve_steps"), sem("skipped"))
        ysum = sem("ysum")
        d = G.dram

        def pair(p, j):
            return G.branch[:, :, :].rearrange("p (b j) d -> p b j d", b=B)[:, 2 * p:2 * p + 2, j, :]

        with nc.Block() as block:
            @block.sync
            def _(sp):
                sp.dma_start(dft[:], d["c_dft"].rearrange("(k p) f -> p k f", p=P)).then_inc(loaded, 16)
                sp.dma_start(inv[:], d["c_inv"].rearrange("(k p) t -> p k t", p=P)).then_inc(loaded, 16)
                sp.dma_start(w[:], d["L1_xattn_W_film_out"].rearrange("(k p) n -> p k n", p=P)).then_inc(loaded, 16)
                sp.dma_start(bias[:], d["L1_xattn_b_film_out"].rearrange("(a n) -> a n", a=1)).then_inc(loaded, 16)
                sp.dma_start(skip[:], d["L1_xattn_D_skip"].partition_broadcast(P)).then_inc(loaded, 16)
                sp.dma_start(gate[:], d["L1_xattn_mod_gate"].partition_broadcast(P)).then_inc(loaded, 16)

            @block.tensor
            def _(pe):
                pe.wait_ge(loaded, 96)
                pe.wait_ge(one, 1)
                for p in range(2):
                    for m in range(FT):
                        n = p * FT + m
                        if n >= 2:
                            pe.wait_ge(xread, n - 1)
                        for c in range(2):
                            for k in range(NT):
                                f = (c * FT + m) * P
                                ins = pe.matmul(pf[n % 2][:, c, :], dft[:, k, f:f + P], pair(p, k),
                                                start=(k == 0), stop=(k == NT - 1))
                        ins.then_inc(xfull, 1)
                    pe.wait_ge(ready, (p + 1) * FT)
                    for j in range(NT):
                        n = p * NT + j
                        if n >= 2:
                            pe.wait_ge(yread, n - 1)
                        for m in range(2 * FT):
                            ins = pe.matmul(py[n % 2][:], inv[:, m, j * P:(j + 1) * P], spec[:, m, :],
                                            start=(m == 0), stop=(m == 2 * FT - 1))
                        ins.then_inc(yfull, 1)
                        for b in range(2):
                            q = 2 * n + b
                            if q >= 2:
                                pe.wait_ge(wread, q - 1)
                            film_product(pe, pw[q % 2], cT, w, ones, bias, (2 * p + b) * NT + j).then_inc(wfull, 1)

            @block.gpsimd
            def _(pool):
                pool.wait_ge(loaded, 96)
                for p in range(2):
                    for m in range(FT):
                        n = p * FT + m
                        pool.wait_ge(xread, n + 1)
                        if p == 1 and m == 0:
                            pool.wait_ge(yfull, NT)
                        pr = prod[:, n % 2]
                        pool.tensor_tensor(spec[:, m, :], pr[:, 0, :], pr[:, 1, :], ALU.subtract)
                        pool.tensor_tensor(spec[:, FT + m, :], pr[:, 2, :], pr[:, 3, :], ALU.add).then_inc(ready, 1)
                    for j in range(NT):
                        n = p * NT + j
                        if n >= 2:
                            pool.wait_ge(ysum, n - 1)
                        pool.tensor_tensor(sk[:, n % 2], pair(p, j), skip[:].unsqueeze(1).to_broadcast([P, 2, D]),
                                           ALU.mult).then_inc(skipped, 1)

            @block.vector
            def _(dve):
                step = chain(dve, dve_steps)
                dve.memset(ones[:], 1.0).then_inc(one, 1)
                dve.wait_ge(loaded, 96)
                for p in range(2):
                    for m in range(FT):
                        n = p * FT + m
                        dve.wait_ge(xfull, n + 1)
                        if n >= 2:
                            dve.wait_ge(ready, n - 1)
                        two = [P, 2, D]
                        kr = kf[:, m, :].unsqueeze(1).to_broadcast(two)
                        ki = kf[:, FT + m, :].unsqueeze(1).to_broadcast(two)
                        for q, (c, kk) in enumerate(((0, kr), (1, ki), (0, ki), (1, kr))):
                            ins = dve.tensor_tensor(prod[:, n % 2, q, :].rearrange("p (b d) -> p b d", b=2),
                                                    pf[n % 2][:, c, :].rearrange("p (b d) -> p b d", b=2), kk, ALU.mult)
                        ins.then_inc(xread, 1)
                    for j in range(NT):
                        n = p * NT + j
                        dve.wait_ge(yfull, n + 1)
                        dve.wait_ge(skipped, n + 1)
                        dve.tensor_tensor(y[:, n % 2], py[n % 2][:].rearrange("p (b d) -> p b d", b=2), sk[:, n % 2],
                                          ALU.add).then_inc(yread, 1)
                        dve.wait_ge(yread, n + 1)
                        dve.sem_inc(ysum, 1)
                        for b in range(2):
                            q = 2 * n + b
                            i = (2 * p + b) * NT + j
                            dve.wait_ge(wfull, q + 1)
                            step(dve.tensor_scalar(s1[:], pw[q % 2][:, 0:D], gate[:, 0:1], 1.0, ALU.mult, ALU.add))
                            dve.tensor_scalar(h1[:], pw[q % 2][:, D:2 * D], gate[:, 0:1], None, ALU.mult
                                              ).then_inc(wread, 1)
                            dve.wait_ge(wread, q + 1)
                            step(dve.tensor_tensor(s1[:], s1[:], y[:, n % 2, b, :], ALU.mult))
                            step(dve.tensor_tensor(s1[:], s1[:], h1[:], ALU.add))
                            step(dve.tensor_tensor(G.branch[:, i, :], s1[:], G.x[:, i, :], ALU.add))


def l1_mlp(nc, G):
    with ExitStack() as ctx:
        sb, ps, sem = buffers(nc, ctx, "ml")
        FD = 4 * D
        FK = FD // P
        w1 = sb("w1", [P, KD, FD])
        w2 = sb("w2", [P, FK, D])
        b1 = sb("b1", [P, FK])
        b2 = sb("b2", [1, D])
        ones = sb("ones", [1, P])
        hT = sb("hT", [P, 2, FK, S])
        ph = [ps(f"ph{i}", [P, S]) for i in range(4)]
        py = [ps(f"py{i}", [P, 512]) for i in range(4)]
        loaded, one, h_full, h_done, y_full, y_done = (
            sem("loaded"), sem("one"), sem("h_full"), sem("h_done"), sem("y_full"), sem("y_done"))
        d = G.dram
        with nc.Block() as block:
            @block.sync
            def _(sp):
                sp.dma_start(w1[:], d["L1_xattn_W1"].rearrange("(k p) n -> p k n", p=P)).then_inc(loaded, 16)
                sp.dma_start(w2[:], d["L1_xattn_W2"].rearrange("(k p) n -> p k n", p=P)).then_inc(loaded, 16)
                with nc.allow_non_contiguous_dma(reason="a bias onto partitions"):
                    sp.dma_start(b1[:], d["L1_xattn_b1"].rearrange("(k p) -> p k", p=P)).then_inc(loaded, 16)
                sp.dma_start(b2[:], d["L1_xattn_b2"].rearrange("(a n) -> a n", a=1)).then_inc(loaded, 16)

            @block.tensor
            def _(pe):
                pe.wait_ge(loaded, 64)
                pe.wait_ge(one, 1)

                def hidden(u):
                    for f in range(FK):
                        n = u * FK + f
                        if n >= 4:
                            pe.wait_ge(h_done, n - 3)
                        for k in range(KD):
                            ins = pe.matmul(ph[n % 4][:], w1[:, k, f * P:(f + 1) * P], G.xT[:, k, u * S:(u + 1) * S],
                                            start=(k == 0), stop=(k == KD - 1))
                        ins.then_inc(h_full, 1)

                def out(u):
                    pe.wait_ge(h_done, (u + 1) * FK)
                    for t in range(NT):
                        n = u * NT + t
                        if n >= 4:
                            pe.wait_ge(y_done, n - 3)
                        for f in range(FK):
                            pe.matmul(py[n % 4][:, 0:D], hT[:, u % 2, f, t * P:(t + 1) * P], w2[:, f, :],
                                      start=(f == 0), stop=False)
                        pe.matmul(py[n % 4][:, 0:D], ones[:], b2[:], start=False, stop=True).then_inc(y_full, 1)

                hidden(0)
                for u in range(B):
                    if u + 1 < B:
                        hidden(u + 1)
                    out(u)

            @block.scalar
            def _(act):
                act.wait_ge(loaded, 64)
                for u in range(B):
                    if u >= 2:
                        act.wait_ge(y_full, (u - 1) * NT)
                    for f in range(FK):
                        n = u * FK + f
                        act.wait_ge(h_full, n + 1)
                        act.activation(hT[:, u % 2, f, :], ph[n % 4][:], ACT.Gelu, bias=b1[:, f:f + 1]
                                       ).then_inc(h_done, 1)

            @block.vector
            def _(dve):
                dve.memset(ones[:], 1.0).then_inc(one, 1)
                for n in range(TT):
                    dve.wait_ge(y_full, n + 1)
                    dve.tensor_tensor(G.branch[:, n, :], py[n % 4][:, 0:D], G.branch[:, n, :], ALU.add
                                      ).then_inc(y_done, 1)


def gain_out(nc, G):
    with ExitStack() as ctx:
        sb, ps, sem = buffers(nc, ctx, "go")
        g = sb("g", [P, D])
        bb = sb("bb", [P, D])
        loaded, dve_steps = sem("loaded"), sem("dve_steps")
        d = G.dram
        with nc.Block() as block:
            @block.sync
            def _(sp):
                sp.dma_start(g[:], d["L1_xattn_g_norm_out"].partition_broadcast(P)).then_inc(loaded, 16)
                sp.dma_start(bb[:], d["L1_xattn_b_norm_out"].partition_broadcast(P)).then_inc(loaded, 16)

            @block.vector
            def _(dve):
                step = chain(dve, dve_steps)
                dve.wait_ge(loaded, 32)
                step(dve.tensor_tensor(G.branch[:], G.branch[:], g[:].unsqueeze(1).to_broadcast([P, TT, D]), ALU.mult))
                dve.tensor_tensor(G.branch[:], G.branch[:], bb[:].unsqueeze(1).to_broadcast([P, TT, D]), ALU.add)


def l1_cross(nc, G):
    d = G.dram
    with ExitStack() as ctx:
        kf = ctx.enter_context(nc.sbuf_tensor("l1_kf", [P, 2 * FT, D], F32))
        s4d_spectrum(nc, G, kf)
        cT = ctx.enter_context(nc.sbuf_tensor("l1_cT", [P, KD, B * S], F32))
        modulation_attention(nc, G, cT)
        norm_stage(nc, G, "ni", add=False, turn=False, dst=G.branch)
        modulate(nc, G, cT)
        convolve(nc, G, cT, kf)
    with ExitStack() as ctx:
        h = ctx.enter_context(nc.sbuf_tensor("l1_h", [P, TT, D], F32))
        norm_stage(nc, G, "nf", add=False, src=G.branch, dst=h, gain=(d["L1_xattn_g_ffn"], d["L1_xattn_b_ffn"]))
    l1_mlp(nc, G)
    norm_stage(nc, G, "no", add=False, turn=False, src=G.branch, dst=G.branch)
    gain_out(nc, G)


E1, F1, TOPE = 64, 64, 8
ES, FS = 2, 512
BF16 = mybir.dt.bfloat16


def l1_ffn(nc, G):
    with ExitStack() as outer:
        weight = outer.enter_context(nc.sbuf_tensor("r1_weight", [P, B * S], BF16))
        low = outer.enter_context(nc.sbuf_tensor("r1_low", [E1, B * S], BF16))
        l1_route(nc, G, weight, low)
        l1_experts(nc, G, weight, low)


def l1_route(nc, G, weight, low):
    with ExitStack() as ctx:
        sb, ps, sem = buffers(nc, ctx, "r1")
        w = sb("w", [P, KD, E1])
        rb = sb("rb", [1, E1])
        b2 = sb("b2", [E1, D])
        sb2 = sb("sb2", [ES, D])
        ones = sb("ones", [ES, P])
        lg = sb("lg", [P, TT, E1])
        e = sb("e", [P, TT, E1])
        rest = sb("rest", [P, TT, E1])
        best = sb("best", [P, TT, 8])
        den = sb("den", [P, TT])
        part = sb("part", [P, TT, 2, E1], BF16)
        two = sb("two", [P, TT, 2, E1])
        last = sb("last", [P, TT, E1])
        cw = sb("cw", [E1, B * S])
        pl = [ps(f"pl{i}", [P, 8, E1]) for i in range(2)]
        pT = [ps(f"pT{i}", [P, NT, P]) for i in range(2)]
        py = [ps(f"py{i}", [P, 512]) for i in range(2)]
        loaded, one, scored, shifted, exped = sem("loaded"), sem("one"), sem("scored"), sem("shifted"), sem("exped")
        weighed, turned, copied, y_full, y_done, dve_steps = (
            sem("weighed"), sem("turned"), sem("copied"), sem("y_full"), sem("y_done"), sem("dve_steps"))
        d = G.dram
        with nc.Block() as block:
            @block.sync
            def _(sp):
                sp.dma_start(w[:], d["L1_ffn_router_w"].rearrange("(k p) n -> p k n", p=P)).then_inc(loaded, 16)
                sp.dma_start(rb[:], d["L1_ffn_router_b"].rearrange("(a n) -> a n", a=1)).then_inc(loaded, 16)
                sp.dma_start(b2[:], d["L1_ffn_b2"]).then_inc(loaded, 16)
                sp.dma_start(sb2[:], d["L1_ffn_sb2"]).then_inc(loaded, 16)

            @block.tensor
            def _(pe):
                pe.wait_ge(loaded, 64)
                pe.wait_ge(one, 1)
                for i in range(TT):
                    out = pl[i // 8][:, i % 8, :]
                    for k in range(KD):
                        pe.matmul(out, G.xT[:, k, i * P:(i + 1) * P], w[:, k, :], start=(k == 0), stop=False)
                    ins = pe.matmul(out, ones[0:1, :], rb[:], start=False, stop=True)
                ins.then_inc(scored, 1)
                pe.wait_ge(weighed, 1)
                for n in range(3 * B):
                    b, kind = n // 3, n % 3
                    if n >= 2:
                        pe.wait_ge(copied, n - 1)
                    for t in range(NT):
                        i = b * NT + t
                        if kind == 0:
                            ins = pe.transpose(pT[n % 2][:, t, :], two[:, i].rearrange("p a e -> p (a e)"), G.ident[:])
                        else:
                            ins = pe.transpose(pT[n % 2][0:E1, t, :], (last, e)[kind - 1][:, i, :], G.ident[:])
                    ins.then_inc(turned, 1)
                pe.wait_ge(copied, 3 * B)
                for i in range(TT):
                    if i >= 2:
                        pe.wait_ge(y_done, i - 1)
                    pe.matmul(py[i % 2][:, 0:D], cw[:, i * P:(i + 1) * P], b2[:], start=True, stop=False)
                    pe.matmul(py[i % 2][:, 0:D], ones[:], sb2[:], start=False, stop=True).then_inc(y_full, 1)

            @block.scalar
            def _(act):
                act.wait_ge(shifted, 1)
                act.activation(e[:], lg[:], ACT.Exp).then_inc(exped, 1)
                for n in range(3 * B):
                    b, kind = n // 3, n % 3
                    act.wait_ge(turned, n + 1)
                    to = (weight, low, cw)[kind][:, b * S:(b + 1) * S]
                    rows = P if kind == 0 else E1
                    act.copy(to, pT[n % 2][0:rows].rearrange("p a b -> p (a b)")).then_inc(copied, 1)

            @block.vector
            def _(dve):
                step = chain(dve, dve_steps)
                dve.memset(ones[:], 1.0).then_inc(one, 1)
                dve.wait_ge(scored, 1)
                for i in range(2):
                    ins = dve.tensor_copy(lg[:, 8 * i:8 * i + 8, :], pl[i][:])
                step(ins)
                for i in range(TT):
                    ins = dve.max(best[:, i, :], lg[:, i, :])
                step(ins)
                for i in range(TT):
                    ins = dve.match_replace(rest[:, i, :], best[:, i, :], lg[:, i, :], GONE)
                step(ins)
                all_ = [P, TT, E1]
                dve.tensor_tensor(lg[:], lg[:], best[:, :, 0:1].to_broadcast(all_), ALU.subtract).then_inc(shifted, 1)
                dve.wait_ge(exped, 1)
                step(dve.scalar_tensor_tensor(e[:], rest[:], GONE, e[:], ALU.is_equal, ALU.mult))
                step(dve.reduce_sum(den[:], e[:], AX.X))
                step(dve.reciprocal(den[:], den[:]))
                step(dve.tensor_tensor(e[:], e[:], den[:].unsqueeze(2).to_broadcast(all_), ALU.mult))
                step(dve.tensor_copy(part[:, :, 0, :], e[:]))
                step(dve.tensor_tensor(rest[:], e[:], part[:, :, 0, :], ALU.subtract))
                step(dve.tensor_copy(part[:, :, 1, :], rest[:]))
                dve.tensor_copy(two[:], part[:])
                dve.tensor_tensor(last[:], rest[:], part[:, :, 1, :], ALU.subtract).then_inc(weighed, 1)
                for i in range(TT):
                    dve.wait_ge(y_full, i + 1)
                    dve.tensor_copy(G.branch[:, i, :], py[i % 2][:, 0:D]).then_inc(y_done, 1)


def l1_experts(nc, G, weight, low):
    with ExitStack() as ctx:
        sb, ps, sem = buffers(nc, ctx, "e1")
        PAIRS, SH = E1 // 2, ES * FS // P
        w1 = sb("w1", [P, KD, E1, F1])
        w2 = sb("w2", [P, PAIRS, D])
        b1 = sb("b1", [P, PAIRS])
        sw1 = sb("sw1", [P, KD, ES, FS])
        sw2 = sb("sw2", [P, SH, D])
        sb1 = sb("sb1", [P, SH])
        spread = sb("spread", [P, E1, F1], BF16)
        act_out = sb("act_out", [P, 3, S])
        hT = sb("hT", [P, 3, S])
        ph = [ps(f"ph{i}", [P, S]) for i in range(2)]
        pc = [ps(f"pc{i}", [P, S]) for i in range(2)]
        py = [ps(f"py{i}", [P, 512]) for i in range(NT)]
        loaded, made = sem("loaded"), sem("made")
        d = G.dram
        ITEMS = PAIRS + SH
        with nc.Block() as block:
            @block.sync
            def _(sp):
                for k in range(KD):
                    sp.dma_start(w1[:, k], d["L1_ffn_w1"].rearrange("e (k p) h -> k p e h", p=P)[k]).then_inc(loaded, 16)
                    for s in range(ES):
                        sp.dma_start(sw1[:, k, s], d["L1_ffn_sw1"][s, k * P:(k + 1) * P, :]).then_inc(loaded, 16)
                sp.dma_start(w2[:], d["L1_ffn_w2"].rearrange("(n a) h d -> (a h) n d", a=2)).then_inc(loaded, 16)
                sp.dma_start(sw2[:], d["L1_ffn_sw2"].rearrange("s (k p) d -> p (s k) d", p=P)).then_inc(loaded, 16)
                with nc.allow_non_contiguous_dma(reason="biases onto partitions"):
                    sp.dma_start(b1[:], d["L1_ffn_b1"].rearrange("(n a) h -> (a h) n", a=2)).then_inc(loaded, 16)
                    sp.dma_start(sb1[:], d["L1_ffn_sb1"].rearrange("s (k p) -> p (s k)", p=P)).then_inc(loaded, 16)
                sp.wait_ge(loaded, 160)

            @block.vector
            def _(dve):
                for half in range(2):
                    r = slice(E1 * half, E1 * half + E1)
                    dve.tensor_copy(spread[r], G.ident[r, r].unsqueeze(2).to_broadcast([E1, E1, F1])).then_inc(made, 1)

        with nc.Fori(0, B) as b, ExitStack() as turn_ctx:
            sem, clear = turn_semaphores(nc, turn_ctx, "e1t")
            h_full, h_done, c_full, ready, used = (
                sem("h_full"), sem("h_done"), sem("c_full"), sem("ready"), sem("used"))
            with nc.Block() as block:
                @block.tensor
                def _(pe):
                    tokens = bass.ds(b * S, S)

                    def hidden(n):
                        if n >= 2:
                            pe.wait_ge(h_done, n - 1)
                        for k in range(KD):
                            m = n - PAIRS
                            lhsT = (w1[:, k, 2 * n:2 * n + 2, :].rearrange("p e h -> p (e h)") if m < 0 else
                                    sw1[:, k, m // 4, (m % 4) * P:(m % 4 + 1) * P])
                            ins = pe.matmul(ph[n % 2][:], lhsT, G.xT[:, k, tokens], start=(k == 0), stop=(k == KD - 1))
                        ins.then_inc(h_full, 1)
                        if n < PAIRS:
                            if n >= 2:
                                pe.wait_ge(ready, n - 1)
                            to = spread[:, 2 * n:2 * n + 2, :].rearrange("p e h -> p (e h)")
                            pe.matmul(pc[n % 2][:], to, weight[:, tokens], start=True, stop=False)
                            pe.matmul(pc[n % 2][:], to[0:E1], low[:, tokens], start=False, stop=True).then_inc(c_full, 1)

                    def out(n):
                        if n < PAIRS:
                            pe.wait_ge(ready, n + 1)
                        else:
                            pe.wait_ge(h_done, n + 1)
                        for t in range(NT):
                            h = hT if n < PAIRS else act_out
                            w = w2[:, n, :] if n < PAIRS else sw2[:, n - PAIRS, :]
                            ins = pe.matmul(py[t][:, 0:D], h[:, n % 3, t * P:(t + 1) * P], w,
                                            start=(n == 0), stop=(n == ITEMS - 1))
                        ins.then_inc(used, 1)

                    for n in range(ITEMS + 2):
                        if n < ITEMS:
                            hidden(n)
                        if n >= 2:
                            out(n - 2)

                @block.scalar
                def _(act):
                    for n in range(ITEMS):
                        act.wait_ge(h_full, n + 1)
                        if n >= 3:
                            if n - 3 < PAIRS:
                                act.wait_ge(ready, n - 2)
                            else:
                                act.wait_ge(used, n - 2)
                        bias = b1[:, n:n + 1] if n < PAIRS else sb1[:, n - PAIRS:n - PAIRS + 1]
                        act.activation(act_out[:, n % 3, :], ph[n % 2][:], ACT.Silu, bias=bias).then_inc(h_done, 1)

                @block.vector
                def _(dve):
                    for n in range(PAIRS):
                        dve.wait_ge(h_done, n + 1)
                        dve.wait_ge(c_full, n + 1)
                        if n >= 3:
                            dve.wait_ge(used, n - 2)
                        dve.tensor_tensor(hT[:, n % 3, :], act_out[:, n % 3, :], pc[n % 2][:], ALU.mult
                                          ).then_inc(ready, 1)
                    dve.wait_ge(used, ITEMS)
                    for t in range(NT):
                        y = G.branch[:, bass.ds(b * NT + t, 1), :].rearrange("p a d -> p (a d)")
                        dve.tensor_tensor(y, py[t][:, 0:D], y, ALU.add)
            clear()


def constants():
    query = np.arange(P)[:, None] % R8
    key = np.arange(R8)[None, :]
    turns = (np.arange(S)[:, None] * (2 * np.arange(FR)[None, :] + 1) % (4 * FR)) / (4 * FR)
    dft = np.concatenate([np.cos(2 * np.pi * turns), -np.sin(2 * np.pi * turns)], 1)
    real = (np.arange(P) < NS)[:, None]
    phase = np.where(real, 0.25, 0.0).astype(np.float32)
    half = np.where(real, [[2.0, 0.0, 0.0, -2.0]], [[0.0, -2.0, -2.0, 0.0]]).astype(np.float32)
    return {"c_ident": np.eye(P, dtype=np.float32), "c_below": np.tril(np.ones((E0, E0), np.float32), -1),
            "c_phase": phase, "c_half": half, "c_low": np.arange(LO, dtype=np.float32),
            "c_high": LO * np.arange(HI, dtype=np.float32), "c_dft": dft.astype(np.float32),
            "c_inv": (dft.T / FR).astype(np.float32).copy(),
            "c_eye8": (query == key).astype(np.float32), "c_cut8": np.where(key > query, HIDE, 0).astype(np.float32)}


def build(nc, dram, out):
    with ExitStack() as ctx:
        G = Shared(nc, ctx, dram)
        G.s4d_positions = nc.dram_tensor("s4d_positions", (P, NT * D), F32).ap()
        load_inputs(nc, G)
        norm_stage(nc, G, "n0", add=False, norm=False)
        stages = [l0_attention, l0_cross, l0_ffn, l1_attention, l1_cross, l1_ffn]
        for i, stage in enumerate(stages):
            stage(nc, G)
            recycle(nc)
            norm_stage(nc, G, f"n{i + 1}", store=out if stage is stages[-1] else None)


def kernel(**inputs):
    import concourse.bacc as bacc
    from concourse.bass_utils import run_bass_kernel_spmd

    nc = bacc.Bacc("TRN2", target_bir_lowering=False, num_devices=1)
    arrays, dram = {}, {}
    given = {k: np.ascontiguousarray(v) for k, v in inputs.items()}
    for name in ("L0_xattn_Wq", "L0_xattn_Wkv", "L0_xattn_Wlkv", "L0_xattn_Wo"):
        given[name + "T"] = np.ascontiguousarray(given.pop(name).T)
    for name in ("A_re", "A_im", "C_re", "C_im"):
        given[f"L1_xattn_{name}T"] = np.ascontiguousarray(given.pop(f"L1_xattn_{name}").T)
    given["L1_attn_mem_kT"] = np.ascontiguousarray(given.pop("L1_attn_mem_k").transpose(0, 2, 1))
    for name, a in (given | constants()).items():
        a = a.reshape(1) if a.ndim == 0 else a
        arrays[f"in_{name}"] = a
        dram[name] = nc.dram_tensor(f"in_{name}", a.shape, U8 if a.dtype == np.bool_ else mybir.dt.from_np(a.dtype), kind="ExternalInput").ap()
    out = nc.dram_tensor("out", (B, S, D), F32, kind="ExternalOutput").ap()
    build(nc, dram, out)
    r = run_bass_kernel_spmd(nc, [arrays], core_ids=[0])
    return r.results[0]["out"]
```
